# Optimizing a Trainium2 kernel written in Bass

```python
import numpy as np
import jax
import jax.numpy as jnp

def _softmax(x, axis=-1):
    return jax.nn.softmax(x, axis=axis)

def _gelu(x):
    return jax.nn.gelu(x, approximate=True)

def _silu(x):
    return jax.nn.silu(x)

def _sigmoid(x):
    return jax.nn.sigmoid(x)

def _layernorm(x, axis=-1, eps=1e-05):
    m = jnp.mean(x, axis=axis, keepdims=True)
    v = jnp.var(x, axis=axis, keepdims=True)
    return (x - m) / jnp.sqrt(v + eps)

def _scatter_add(tgt, idx, src, axis=0):
    return tgt.at[idx].add(src)

def _segment_sum(src, seg, n):
    return jax.ops.segment_sum(src, seg, n)
kernel_name = 'mk_recurrent_d1_jaxref_r8_2fecbe'

def setup_inputs(seed: int=0):
    np.random.seed(seed)
    _w = jnp.asarray

    def _L0_attn_setup():
        import jax, jax.numpy as jnp
        import numpy as np
        D = 128
        H = 16
        HD = D // H
        EPS = 1e-06

        def rms_norm(x, w):
            xf = x.astype(jnp.float32)
            rms = jnp.sqrt(jnp.mean(xf * xf, axis=-1, keepdims=True) + EPS)
            return (xf / rms * w.astype(jnp.float32)).astype(x.dtype)
        key = jax.random.key(seed)
        ks = jax.random.split(key, 6)
        B, S = (2, 256)
        x = jax.random.normal(ks[0], (B, S, D), dtype=jnp.float32)
        Wqkv = jax.random.normal(ks[1], (3 * D, D), dtype=jnp.float32) * (1.0 / np.sqrt(D))
        bqkv = jax.random.normal(ks[2], (3 * D,), dtype=jnp.float32) * 0.02
        Wproj = jax.random.normal(ks[3], (D, D), dtype=jnp.float32) * (1.0 / np.sqrt(D))
        bproj = jax.random.normal(ks[4], (D,), dtype=jnp.float32) * 0.02
        qn_w = jnp.ones((HD,), dtype=jnp.float32)
        kn_w = jnp.ones((HD,), dtype=jnp.float32)
        return {'x': x, 'Wqkv': Wqkv, 'bqkv': bqkv, 'Wproj': Wproj, 'bproj': bproj, 'qn_w': qn_w, 'kn_w': kn_w}
    _L0_attn_in = _L0_attn_setup()

    def _L0_ffn_setup():
        import jax, jax.numpy as jnp
        import numpy as np
        DIM = 128
        HIDDEN = 384
        SCALE = 1.0 / 127.0

        def _dequant(w_int, dtype):
            return w_int.astype(dtype) * jnp.asarray(SCALE, dtype)
        key = jax.random.key(seed)
        k_x, k_g, k_u, k_d = jax.random.split(key, 4)
        x = jax.random.normal(k_x, (4, 256, DIM), dtype=jnp.float32)
        w_gate = jax.random.randint(k_g, (HIDDEN, DIM), -127, 128, dtype=jnp.int32)
        w_up = jax.random.randint(k_u, (HIDDEN, DIM), -127, 128, dtype=jnp.int32)
        w_down = jax.random.randint(k_d, (DIM, HIDDEN), -127, 128, dtype=jnp.int32)
        return {'x': x, 'w_gate': w_gate, 'w_up': w_up, 'w_down': w_down}
    _L0_ffn_in = _L0_ffn_setup()
    _d = {'L0_attn_x': _L0_attn_in['x'], 'L0_attn_Wqkv': _L0_attn_in['Wqkv'], 'L0_attn_bqkv': _L0_attn_in['bqkv'], 'L0_attn_Wproj': _L0_attn_in['Wproj'], 'L0_attn_bproj': _L0_attn_in['bproj'], 'L0_attn_qn_w': _L0_attn_in['qn_w'], 'L0_attn_kn_w': _L0_attn_in['kn_w'], 'L0_ffn_w_gate': _L0_ffn_in['w_gate'], 'L0_ffn_w_up': _L0_ffn_in['w_up'], 'L0_ffn_w_down': _L0_ffn_in['w_down']}
    _x0 = _d['L0_attn_x']
    _d['L0_attn_x'] = jax.random.normal(jax.random.fold_in(jax.random.key(seed), 1), (4, 1024, 128), dtype=_x0.dtype)
    del _x0
    return _d

def reference(L0_attn_x, L0_attn_Wqkv, L0_attn_bqkv, L0_attn_Wproj, L0_attn_bproj, L0_attn_qn_w, L0_attn_kn_w, L0_ffn_w_gate, L0_ffn_w_up, L0_ffn_w_down):

    def _L0_attn_ref(x, Wqkv, bqkv, Wproj, bproj, qn_w, kn_w):
        import jax, jax.numpy as jnp
        import numpy as np
        D = 128
        H = 16
        HD = D // H
        EPS = 1e-06

        def rms_norm(x, w):
            xf = x.astype(jnp.float32)
            rms = jnp.sqrt(jnp.mean(xf * xf, axis=-1, keepdims=True) + EPS)
            return (xf / rms * w.astype(jnp.float32)).astype(x.dtype)
        B, S, _ = x.shape
        qkv = x @ Wqkv.T + bqkv
        qkv = qkv.reshape(B, S, 3, H, HD)
        q, k, v = (qkv[:, :, 0], qkv[:, :, 1], qkv[:, :, 2])
        q = rms_norm(q, qn_w)
        k = rms_norm(k, kn_w)
        q = q.transpose(0, 2, 1, 3)
        k = k.transpose(0, 2, 1, 3)
        v = v.transpose(0, 2, 1, 3)
        scale = 1.0 / np.sqrt(HD)
        scores = jnp.einsum('bhsd,bhtd->bhst', q, k) * scale
        attn = jax.nn.softmax(scores, axis=-1)
        out = jnp.einsum('bhst,bhtd->bhsd', attn, v)
        out = out.transpose(0, 2, 1, 3).reshape(B, S, D)
        return out @ Wproj.T + bproj

    def _L0_ffn_ref(x, w_gate, w_up, w_down):
        import jax, jax.numpy as jnp
        import numpy as np
        DIM = 128
        HIDDEN = 384
        SCALE = 1.0 / 127.0

        def _dequant(w_int, dtype):
            return w_int.astype(dtype) * jnp.asarray(SCALE, dtype)
        wg = _dequant(w_gate, x.dtype)
        wu = _dequant(w_up, x.dtype)
        wd = _dequant(w_down, x.dtype)
        gate = jnp.einsum('bsd,hd->bsh', x, wg)
        up = jnp.einsum('bsd,hd->bsh', x, wu)
        h = jax.nn.silu(gate) * up
        return jnp.einsum('bsh,dh->bsd', h, wd)
    x = L0_attn_x
    xn = _layernorm(x, axis=-1)
    s = _L0_attn_ref(xn, L0_attn_Wqkv, L0_attn_bqkv, L0_attn_Wproj, L0_attn_bproj, L0_attn_qn_w, L0_attn_kn_w)
    g = _silu(_L0_ffn_ref(xn, L0_ffn_w_gate, L0_ffn_w_up, L0_ffn_w_down))
    x = x + s * g
    return x

_drawn_inputs = setup_inputs


def setup_inputs(seed=0):
    import zlib

    import numpy as np

    out = dict(_drawn_inputs(seed))
    spreads = {'L0_attn_qn_w': (1.0, 0.2), 'L0_attn_kn_w': (1.0, 0.2)}
    factors = {}
    for name, (base, spread) in spreads.items():
        noise = np.random.default_rng([zlib.crc32(name.encode()), seed]).standard_normal(out[name].shape)
        drawn = base * np.exp(spread * noise) if base else spread * noise
        out[name] = jnp.asarray(drawn.astype(out[name].dtype))
    for name, factor in factors.items():
        out[name] = (out[name] * factor).astype(out[name].dtype)
    return out
```

```python
from contextlib import ExitStack

import concourse.bass as bass
from concourse import mybir

F32 = mybir.dt.float32
BF16 = mybir.dt.bfloat16
I32 = mybir.dt.int32
U32 = mybir.dt.uint32
ALU = mybir.AluOpType
ACT = mybir.ActivationFunctionType
AX_X = mybir.AxisListType.X
AX_XY = mybir.AxisListType.XY

P = 128
D = 128
H = 16
HD = D // H
HIDDEN = 384
HC = HIDDEN // P
B, S = 4, 1024
UNIT = 512
T = UNIT // P
UNITS = B * S // UNIT
QUADS = H // 4
KT = S // P
STEPS = QUADS * KT
GROUPS = 2 * STEPS
PARTS = 3
ROWS = PARTS * PARTS * HD
KROWS = ROWS + PARTS
SRING = 3
PRING = 8
VW = 32
LN_EPS = 1e-5
RMS_EPS = 1e-6
W_SCALE = 1.0 / 127.0
SCORE_SCALE = HD ** -0.5
SAFE_BOUND = 60.0
RSQRT_MAGIC = 1597463007.0

POST_JOBS = [(1, "heads", 3), (2, "attnT", 0), (3, "proj", 0)]
HEAD_JOBS = [(9, "heads", 0), (17, "heads", 1), (25, "heads", 2)]
PREP_JOBS = [(4, "xT", 0), (5, "qkv", 0), (6, "qkv", 1), (7, "qkv", 2), (8, "qkv", 3), (19, "kT", 1), (21, "qT", 0)]
FFN_JOBS = [(10, "gate", 0), (11, "gate", 1), (12, "gate", 2), (16, "up", 0), (18, "up", 1), (23, "up", 2),
            (27, "down", 0)]
TANH_GATE_GROUP = 30
TANH_Y_GROUP = 60
RMS_STEPS = {11: 0, 12: 1, 13: 2, 14: 3, 15: 4}


class Jobs:
    def __init__(self, jobs, before):
        self.order = [(name, arg) for _, name, arg in sorted(jobs)]
        self.steps = [step for step, _, _ in sorted(jobs)]
        self.before = before

    def free(self, name, arg=0):
        return self.before + self.order.index((name, arg))

    def filled(self, name, arg=0):
        return self.before + self.order.index((name, arg)) + 1

    def at(self, step):
        return [job for job, s in zip(self.order, self.steps) if s == step]


def jobs_of(post, prep, before):
    return Jobs(HEAD_JOBS + POST_JOBS * post + (PREP_JOBS + FFN_JOBS) * prep, before)


N_PREP, N_FFN, N_POST, N_HEADS = len(PREP_JOBS), len(FFN_JOBS), len(POST_JOBS), len(HEAD_JOBS)
N_NEXT = N_PREP + N_FFN
LAST_JOBS = Jobs(POST_JOBS, N_PREP + (UNITS - 2) * N_NEXT + UNITS * N_HEADS + (UNITS - 1) * N_POST)


def slot_of(g):
    return 1 if g == GROUPS - 1 else g % SRING


def last_user(g):
    slot = slot_of(g)
    return next(k for k in range(g - 1, g - 6, -1) if slot_of(k % GROUPS) == slot)


def attention_ffn(nc, x, WqkvT, bqkv, WprojT, bproj, qn_w, kn_w, w_gateT, w_upT, w_downT, out, force_general=False):
    with ExitStack() as ctx:
        def sb(name, shape, dt=F32):
            return ctx.enter_context(nc.sbuf_tensor(name, shape, dt))

        def sem(name):
            return ctx.enter_context(nc.semaphore(name))

        q_rows = nc.dram_tensor("q_rows", (UNITS, PARTS, PARTS, HD, H, UNIT), BF16, kind="Internal").ap()
        k_rows = nc.dram_tensor("k_rows", (B, PARTS, HD, H, S), BF16, kind="Internal").ap()
        shifts = nc.dram_tensor("shifts", (UNITS, PARTS, H, UNIT), BF16, kind="Internal").ap()

        scores = ctx.enter_context(nc.psum_tensor("scores", [P, SRING, 2, 512], F32))
        heads_o = ctx.enter_context(nc.psum_tensor("heads_o", [P, UNIT], F32))
        misc = ctx.enter_context(nc.psum_tensor("misc", [P, 512], F32))

        x_all = sb("x_all", [P, UNITS * T, D])
        g2_all = sb("g2_all", [P, UNITS * T, D])
        v_all = sb("v_all", [P, UNITS * T, D])
        k_ring = sb("k_ring", [KROWS, QUADS, 4, S], BF16)
        q_ring = sb("q_ring", [KROWS, QUADS, 4, UNIT], BF16)
        v_ring = sb("v_ring", [P, QUADS, KT, 4, VW])
        probs = sb("probs", [P, PRING, 2, UNIT])
        ident = sb("ident", [P, P])
        wqkv = sb("wqkv", [P, 3 * D])
        bqkv_b = sb("bqkv_b", [P, 3 * D])
        wproj = sb("wproj", [P, D])
        bproj_b = sb("bproj_b", [P, D])
        norm_w = sb("norm_w", [P, 2])
        norm_rows = sb("norm_rows", [1, 2, HD])
        bound = sb("bound", [1, HD + 2])
        unsafe = sb("unsafe", [1, 1], I32)
        w_ffn = sb("w_ffn", [P, 3, HIDDEN])
        early = probs[:].rearrange("p a b c -> p (a b c)")
        w_int = early[:, 0:3 * HIDDEN].bitcast(I32).rearrange("p (w h) -> p w h", w=3)
        zero_words = UNITS * PARTS * H * UNIT // P // 2
        zeros = early[:, 3 * HIDDEN:3 * HIDDEN + zero_words]
        early_at = [3 * HIDDEN + zero_words]
        stats = sb("stats", [P, UNITS * T, 6])
        mv = sb("mv", [P, UNITS * T, 2])
        ln_r = sb("ln_r", [P, UNITS * T])
        rs_x = sb("rs_x", [P, 2, P])
        rs_y = sb("rs_y", [P, 2, P])
        rs_t = sb("rs_t", [P, 2, P])

        def early_room(name, shape, dt=F32):
            words = 1
            for n in shape[1:]:
                words *= n
            words = words * (2 if dt is BF16 else 4) // 4
            at = early_at[0]
            early_at[0] += words
            flat = early[:, at:at + words]
            flat = flat.bitcast(BF16) if dt is BF16 else flat
            if len(shape) == 3:
                return flat.rearrange("p (a b) -> p a b", a=shape[1])
            if len(shape) == 4:
                return flat.rearrange("p (a b c) -> p a b c", a=shape[1], b=shape[2])
            return flat

        class Workspace:
            def __init__(self, tag, room, bank, n, parts=None):
                self.bank = bank
                self.xn = room(tag + "xn", [P, T, D])
                self.xT = room(tag + "xT", [P, UNIT])
                self.qk = room(tag + "qk", [P, T, 2 * D])
                self.sq = room(tag + "sq", [P, T, 2 * D])
                self.qkn = self.sq
                self.full = room(tag + "full", [P, UNIT])
                self.rest = room(tag + "rest", [P, UNIT])
                self.parts = room(tag + "parts", [P, 2, PARTS, UNIT], BF16) if parts is None else parts
                self.rs_t, self.rs_y = rs_t[:, n, :], rs_y[:, n, :]
        gate = sb("gate", [P, HC, UNIT])
        tanh_gate = sb("tanh_gate", [P, HC, UNIT])
        y = sb("y", [P, UNIT])
        tanh_y = sb("tanh_y", [P, UNIT])
        o_sb = sb("o_sb", [P, UNIT])
        denom_r = sb("denom_r", [P, T * 4])
        post_room = sb("post_room", [P, 3, UNIT])
        attn = post_room[:, 0, :].rearrange("p (t c) -> p t c", t=T)
        attnT, joined = post_room[:, 1, :], post_room[:, 2, :]
        second_parts = post_room[:].rearrange("p a b -> p (a b)").bitcast(BF16).rearrange(
            "p (m c s) -> p m c s", m=2, c=PARTS)
        joined_x = sb("joined_x", [P, T, D])
        row_max = sb("row_max", [P, T])
        shift_rest = sb("shift_rest", [P, T])
        shift_parts = sb("shift_parts", [P, PARTS, T], BF16)

        class Sems:
            def __init__(self, tag):
                self.filled = sem(tag + "filled")
                self.free = sem(tag + "free")
                self.xn_ready = sem(tag + "xn_ready")
                self.sq_ready = sem(tag + "sq_ready")
                self.rms_ready = sem(tag + "rms_ready")
                self.qkn_ready = sem(tag + "qkn_ready")
                self.k_split = sem(tag + "k_split")
                self.q_split = sem(tag + "q_split")
                self.k_stored = sem(tag + "k_stored")
                self.q_stored = sem(tag + "q_stored")

        def tile(name, shape, dt=F32):
            return sb(name, shape, dt)[:]

        misc_ap = misc[:]
        first_ws = Workspace("a_", tile, misc_ap, 0)
        second_ws = Workspace("b_", early_room, scores[:, 0, 0, :], 1, second_parts)
        assert early_at[0] <= PRING * 2 * UNIT
        ffn_bank = scores[:, 0, 1, :]
        main = Sems("")
        second = Sems("b_")
        general = Sems("g_")
        ffn_filled = sem("ffn_filled")
        ffn_free = sem("ffn_free")
        w_loaded = sem("w_loaded")
        ffn_loaded = sem("ffn_loaded")
        x_first = sem("x_first")
        x_rest = sem("x_rest")
        ident_zero = sem("ident_zero")
        ident_ready = sem("ident_ready")
        ring_set = sem("ring_set")
        ones_set = sem("ones_set")
        zeros_set = sem("zeros_set")
        w_ready = sem("w_ready")
        bound_ready = sem("bound_ready")
        shifts_zero = sem("shifts_zero")
        kq_loaded = [sem(f"kq_loaded{q}") for q in range(QUADS)]
        v_loaded = [sem(f"v_loaded{q}") for q in range(QUADS)]
        v_turns = sem("v_turns")
        scores_ready = sem("scores_ready")
        probs_ready = sem("probs_ready")
        probs_used = sem("probs_used")
        o_free = sem("o_free")
        tanh_done = sem("tanh_done")
        out_ready = sem("out_ready")
        out_stored = sem("out_stored")
        g_loaded = sem("g_loaded")
        g_scores = sem("g_scores")
        g_max = sem("g_max")
        g_shift = sem("g_shift")
        g_stored = sem("g_stored")
        g_over = sem("g_over")

        K_STORED = PARTS * 16
        Q_STORED = PARTS * PARTS * 16
        W_DMAS = 6
        FFN_DMAS = 5
        HEAD_DMAS = PARTS + 1
        KQ_DMAS = PARTS + 2
        ENGINES = 5

        x_v = x.rearrange("b (t p) c -> p (b t) c", p=P)
        out_v = out.rearrange("b (u t p) c -> (b u) p t c", p=P, t=T)

        def need(engine, semaphore, value):
            if not isinstance(value, int) or value > 0:
                engine.wait_ge(semaphore, value)

        block = ctx.enter_context(nc.Block())

        def run_bodies(engine, body):
            before = N_PREP
            body(0, jobs_of(0, 1, before), post=False, prep=True, first=True)
            before += N_HEADS + N_NEXT
            step = N_HEADS + N_NEXT + N_POST
            with engine.Fori(0, UNITS - 3) as k:
                body(k + 1, jobs_of(1, 1, k * step + before), post=True, prep=True, first=False)
            before += (UNITS - 3) * step
            step = N_HEADS + N_POST
            with engine.Fori(0, 2) as k:
                body(k + UNITS - 2, jobs_of(1, 0, k * step + before), post=True, prep=False, first=False)

        prep_jobs = Jobs(PREP_JOBS, 0)
        ffn_jobs = [Jobs(FFN_JOBS, 0), Jobs(FFN_JOBS, N_FFN)]

        def general_path(engine, run):
            engine.wait_ge(bound_ready, 1)
            flag = engine.value_load(unsafe[0:1, 0:1], min_val=0, max_val=1)
            with engine.If(flag > 0):
                run()
                engine.wait_ge(g_over, ENGINES)

        @block.sync
        def _(sp):
            for u in range(UNITS):
                sp.dma_start(x_all[:, u * T:(u + 1) * T, :], x_v[:, u * T:(u + 1) * T, :]).then_inc(
                    x_first if u < 2 else x_rest, 16)
            sp.wait_ge(zeros_set, 1)
            sp.dma_start(shifts.rearrange("u a h s -> (u a h s)").rearrange("(p f) -> p f", p=P),
                         zeros.bitcast(BF16)).then_inc(shifts_zero, 16)

            def store_k(u, p, ws, s):
                sp.wait_ge(s.k_split, p + 1)
                for c in range(PARTS):
                    dst = k_rows[bass.ds(u // 2, 1), c, :, :, bass.ds(u % 2 * UNIT, UNIT)]
                    sp.dma_start(dst.rearrange("b d h s -> h d (b s)"), ws.parts[:, 1, c, :]).then_inc(s.k_stored, 16)

            def store_q(u, p, ws, s):
                sp.wait_ge(s.q_split, p + 1)
                for r in range(PARTS):
                    for c in range(PARTS):
                        dst = q_rows[bass.ds(u, 1), r, c, :, :, :]
                        sp.dma_start(dst.rearrange("u d h s -> h d (u s)"), ws.parts[:, 0, r, :]
                                     ).then_inc(s.q_stored, 16)

            def load_heads(i, heads, slot, n, done):
                for r in range(PARTS):
                    src = k_rows[bass.ds(i // 2, 1), :, :, heads, :].rearrange("b c d h s -> (b c d) h s")
                    sp.dma_start(k_ring[r * PARTS * HD:(r + 1) * PARTS * HD, slot, 0:n, :], src).then_inc(done, 16)
                src = q_rows[bass.ds(i, 1), :, :, :, heads, :].rearrange("u r c d h s -> (u r c d) h s")
                sp.dma_start(q_ring[0:ROWS, slot, 0:n, :], src).then_inc(done, 16)

            def load_quads(i, first=False):
                for q in range(QUADS):
                    if not first:
                        sp.wait_ge(probs_used, (i - 1) * STEPS + KT * (q + 1))
                    load_heads(i, slice(4 * q, 4 * q + 4), q, 4, kq_loaded[q])
                    sp.dma_start(q_ring[ROWS:KROWS, q, :, :], shifts[bass.ds(i, 1), :, 4 * q:4 * q + 4, :].rearrange(
                        "u a h s -> (u a) h s")).then_inc(kq_loaded[q], 16)

            def store_out(i):
                sp.wait_ge(out_ready, i + 1)
                sp.dma_start(out_v[bass.ds(i, 1)].rearrange("a p t c -> p (a t) c"), joined_x[:]).then_inc(out_stored, 16)

            sp.wait_ge(shifts_zero, 16)

            def run_general():
                with sp.Fori(0, UNITS) as u:
                    store_k(u, u, first_ws, general)
                    store_q(u, u, first_ws, general)
                sp.wait_ge(general.k_stored, UNITS * K_STORED)
                sp.wait_ge(general.q_stored, UNITS * Q_STORED)
                with sp.Fori(0, UNITS) as u:
                    with sp.Fori(0, H) as h:
                        n = u * H + h
                        load_heads(u, bass.ds(h, 1), 0, 1, g_loaded)
                        sp.wait_ge(g_shift, n + 1)
                        dst = shifts[bass.ds(u, 1), :, bass.ds(h, 1), :].rearrange("u a h (t p) -> p (u a h) t", p=P)
                        for a in range(PARTS):
                            sp.dma_start(dst[:, a, :], shift_parts[:, a, :], allow_slow_non_contiguous=True
                                         ).then_inc(g_stored, 16)
                sp.wait_ge(g_stored, UNITS * H * PARTS * 16)
                sp.drain().then_inc(g_over, 1)

            general_path(sp, run_general)

            store_k(0, 0, first_ws, main)
            store_k(1, 0, second_ws, second)
            store_q(0, 0, first_ws, main)
            sp.wait_ge(main.k_stored, K_STORED)
            sp.wait_ge(second.k_stored, K_STORED)
            sp.wait_ge(main.q_stored, Q_STORED)
            sp.wait_ge(ones_set, 1)
            load_quads(0, first=True)
            store_q(1, 0, second_ws, second)

            def body(i, jobs, post, prep, first):
                if not first:
                    sp.wait_ge(main.k_stored, (i + 1) * K_STORED if prep else (UNITS - 1) * K_STORED)
                    sp.wait_ge(main.q_stored, i * Q_STORED)
                    load_quads(i)
                if post:
                    store_out(i - 1)
                if prep:
                    store_k(i + 2, i + 1, first_ws, main)
                    store_q(i + 2, i + 1, first_ws, main)

            run_bodies(sp, body)
            store_out(UNITS - 1)
            sp.wait_ge(out_stored, UNITS * 16)
            sp.wait_ge(main.k_stored, (UNITS - 1) * K_STORED)
            sp.wait_ge(main.q_stored, (UNITS - 1) * Q_STORED)

        @block.gpsimd
        def _(pool):
            nc.gpsimd.memset(ident[:], 0.0).then_inc(ident_zero, 1)
            pool.wait_ge(ident_zero, 1)
            nc.gpsimd.affine_select(out=ident[:], in_=ident[:], compare_op=ALU.not_equal, fill=1.0, base=0,
                                    pattern=[[-1, P]], channel_multiplier=1).then_inc(ident_ready, 1)

            pool.wait_ge(ident_ready, 1)
            nc.gpsimd.memset(k_ring[64:KROWS, :, :, :].bitcast(U32), 0x3F803F80).then_inc(ring_set, 1)
            pool.wait_ge(ring_set, 1)
            nc.gpsimd.memset(v_ring[:], 0.0).then_inc(ring_set, 1)
            pool.wait_ge(ring_set, 2)
            nc.gpsimd.memset(v_ring[:, :, :, :, HD:HD + 1], 1.0).then_inc(ones_set, 1)

            def square(jobs, ws, s):
                pool.wait_ge(s.free, jobs.filled("qkv", T - 1))
                nc.gpsimd.tensor_tensor(ws.sq, ws.qk, ws.qk, ALU.mult).then_inc(s.sq_ready, 1)

            def norm(p, ws, s):
                pool.wait_ge(s.rms_ready, p + 1)
                heads = ws.qk.rearrange("p t (h d) -> p (t h) d", d=HD)
                nc.gpsimd.tensor_tensor(ws.qkn.rearrange("p t (h d) -> p (t h) d", d=HD), heads,
                                        ws.rs_y.unsqueeze(2).broadcast_to(heads.shape), ALU.mult
                                        ).then_inc(s.qkn_ready, 1)

            def load_v(i, first):
                for q in range(QUADS):
                    if not first:
                        pool.wait_ge(probs_used, (i - 1) * STEPS + KT * (q + 1))
                        pool.sem_inc(v_turns, 1)
                    for t in range(KT):
                        src = v_all[:, bass.ds(i // 2 * KT + t, 1), 4 * q * HD:4 * (q + 1) * HD]
                        move = nc.gpsimd.tensor_copy(v_ring[:, q, t, :, 0:HD],
                                                     src.rearrange("p t (h d) -> p (t h) d", d=HD))
                    move.then_inc(v_loaded[q], 1)

            def run_general():
                with pool.Fori(0, UNITS) as u:
                    square(Jobs(PREP_JOBS, u * N_PREP), first_ws, general)
                    norm(u, first_ws, general)
                pool.drain().then_inc(g_over, 1)

            general_path(pool, run_general)

            pool.wait_ge(second.free, prep_jobs.filled("qkv", T - 1))
            norm(0, first_ws, main)
            norm(0, second_ws, second)

            def body(i, jobs, post, prep, first):
                load_v(i, first)
                if prep:
                    square(jobs, first_ws, main)
                    norm(i + 1, first_ws, main)

            run_bodies(pool, body)

        @block.tensor
        def _(pe):
            def transposed(bank, tiles):
                for t, tile in enumerate(tiles):
                    last = nc.tensor.transpose(bank[:, t * P:(t + 1) * P], tile, ident[:])
                return last

            def prep_job(name, arg, p, jobs, ws, s):
                need(pe, s.free, jobs.free(name, arg))
                if name == "xT":
                    pe.wait_ge(s.xn_ready, p + 1)
                    last = transposed(ws.bank, [ws.xn[:, t, :] for t in range(T)])
                elif name == "qkv":
                    last = nc.tensor.matmul(ws.bank[:, 0:3 * D], ws.xT[:, arg * P:(arg + 1) * P], wqkv[:],
                                            start=True, stop=True)
                else:
                    if name == "kT":
                        pe.wait_ge(s.qkn_ready, p + 1)
                    last = transposed(ws.bank, [ws.qkn[:, t, arg * D:(arg + 1) * D] for t in range(T)])
                last.then_inc(s.filled, 1)

            def ffn_job(name, arg, jobs, bank, ws, free, filled):
                need(pe, free, jobs.free(name, arg))
                if name == "down":
                    for t in range(T):
                        for c in range(HC):
                            last = nc.tensor.matmul(bank[:, t * D:(t + 1) * D], gate[:, c, t * P:(t + 1) * P],
                                                    w_ffn[:, 2, c * D:(c + 1) * D], start=c == 0, stop=c == HC - 1)
                else:
                    w = w_ffn[:, 0 if name == "gate" else 1, arg * P:(arg + 1) * P]
                    last = nc.tensor.matmul(bank, w, ws.xT, start=True, stop=True)
                last.then_inc(filled, 1)

            def post_job(name, arg, i, jobs):
                need(pe, main.free, jobs.free(name, arg))
                if name == "heads":
                    pe.wait_ge(o_free, i * QUADS if arg == QUADS - 1 else i * QUADS + arg + 1)
                    last = transposed(misc_ap, [o_sb[:, t * P:(t + 1) * P] for t in range(T)])
                elif name == "attnT":
                    last = transposed(misc_ap, [attn[:, t, :] for t in range(T)])
                else:
                    for t in range(T):
                        last = nc.tensor.matmul(misc[:, t * D:(t + 1) * D], attnT[:, t * P:(t + 1) * P], wproj[:],
                                                start=True, stop=True)
                last.then_inc(main.filled, 1)

            pe.wait_ge(ident_ready, 1)
            pe.wait_ge(w_loaded, W_DMAS * 16)

            def run_general():
                with pe.Fori(0, UNITS) as u:
                    jobs = Jobs(PREP_JOBS, u * N_PREP)
                    for name, arg in jobs.order:
                        prep_job(name, arg, u, jobs, first_ws, general)
                with pe.Fori(0, UNITS * H) as n:
                    pe.wait_ge(g_loaded, (n + 1) * (HEAD_DMAS * 16))
                    for t in range(T):
                        if t < 2:
                            pe.wait_ge(g_shift, n)
                        else:
                            pe.wait_ge(g_max, n * T + t - 1)
                        for half in range(2):
                            last = nc.tensor.matmul(scores[:, t % 2, half, :], q_ring[0:ROWS, 0, 0, t * P:(t + 1) * P],
                                                    k_ring[0:ROWS, 0, 0, half * 512:(half + 1) * 512],
                                                    start=True, stop=True)
                        last.then_inc(g_scores, 1)
                pe.drain().then_inc(g_over, 1)

            general_path(pe, run_general)

            def both(name, arg):
                prep_job(name, arg, 0, prep_jobs, first_ws, main)
                prep_job(name, arg, 0, prep_jobs, second_ws, second)

            def early_ffn(unit, names):
                for name, arg in ffn_jobs[unit].order:
                    if name in names:
                        ffn_job(name, arg, ffn_jobs[unit], ffn_bank, (first_ws, second_ws)[unit], ffn_free, ffn_filled)

            both("xT", 0)
            for t in range(T):
                both("qkv", t)
            pe.wait_ge(w_ready, 1)
            early_ffn(0, ["gate"])
            both("kT", 1)
            both("qT", 0)
            early_ffn(0, ["up", "down"])
            early_ffn(1, ["gate", "up", "down"])

            def score_group(g, i, first):
                q, t, pair = g // (2 * KT), g // 2 % KT, g % 2
                if g % (2 * KT) == 0:
                    pe.wait_ge(kq_loaded[q], (i + 1) * (KQ_DMAS * 16))
                if not first or last_user(g) >= 0:
                    pe.wait_ge(probs_ready, i * GROUPS + last_user(g) + 1)
                for k in range(2):
                    j = 2 * pair + k
                    last = nc.tensor.matmul(scores[:, slot_of(g), k, :], k_ring[:, q, j, t * P:(t + 1) * P],
                                            q_ring[:, q, j, :], start=True, stop=True)
                last.then_inc(scores_ready, 1)

            def weigh_v(n, i):
                q, t = n // KT, n % KT
                if t == 0:
                    pe.wait_ge(v_loaded[q], i + 1)
                    need(pe, o_free, i * QUADS + q)
                pe.wait_ge(probs_ready, i * GROUPS + 2 * n + 2)
                for j in range(4):
                    last = nc.tensor.matmul(heads_o[j * VW:(j + 1) * VW, :], v_ring[:, q, t, j, :],
                                            probs[:, (2 * n + j // 2) % PRING, j % 2, :],
                                            start=t == 0, stop=t == KT - 1)
                last.then_inc(probs_used, 1)

            def body(i, jobs, post, prep, first):
                if first:
                    pe.wait_ge(second.free, N_PREP)
                    pe.wait_ge(ffn_free, 2 * N_FFN)
                score_group(0, i, first)
                for n in range(STEPS):
                    score_group(2 * n + 1, i, first)
                    if n < STEPS - 1:
                        score_group(2 * n + 2, i, first)
                    if n > 0:
                        weigh_v(n - 1, i)
                    elif post:
                        weigh_v(STEPS - 1, i - 1)
                    for name, arg in jobs.at(n):
                        if (n, name, arg) in PREP_JOBS:
                            prep_job(name, arg, i + 1, jobs, first_ws, main)
                        elif (n, name, arg) in FFN_JOBS:
                            ffn_job(name, arg, jobs, misc_ap, first_ws, main.free, main.filled)
                        else:
                            post_job(name, arg, i, jobs)

            run_bodies(pe, body)
            weigh_v(STEPS - 1, UNITS - 1)
            for name, arg in LAST_JOBS.order:
                post_job(name, arg, UNITS, LAST_JOBS)

        @block.scalar
        def _(act):
            act.dma_start(norm_rows[0:1, 0, :], qn_w[0:1, 0:HD]).then_inc(w_loaded, 16)
            act.dma_start(norm_rows[0:1, 1, :], kn_w[0:1, 0:HD]).then_inc(w_loaded, 16)
            act.dma_start(wqkv[:], WqkvT).then_inc(w_loaded, 16)
            act.dma_start(bqkv_b[:], bqkv.partition_broadcast(P)).then_inc(w_loaded, 16)
            act.dma_start(norm_w[:, 0:1], qn_w.rearrange("a p -> p a")).then_inc(w_loaded, 16)
            act.dma_start(norm_w[:, 1:2], kn_w.rearrange("a p -> p a")).then_inc(w_loaded, 16)
            act.dma_start(w_int[:, 0, :], w_gateT).then_inc(ffn_loaded, 16)
            act.dma_start(w_int[:, 1, :], w_upT).then_inc(ffn_loaded, 16)
            act.dma_start(w_int[:, 2, :], w_downT).then_inc(ffn_loaded, 16)
            act.dma_start(wproj[:], WprojT).then_inc(ffn_loaded, 16)
            act.dma_start(bproj_b[:], bproj.partition_broadcast(P)).then_inc(ffn_loaded, 16)

            def run_general():
                act.drain().then_inc(g_over, 1)

            general_path(act, run_general)

            def square(ws, s):
                act.wait_ge(s.free, prep_jobs.filled("qkv", T - 1))
                nc.scalar.activation(ws.sq, ws.qk, ACT.Square).then_inc(s.sq_ready, 1)

            def gate_tanh(jobs, free):
                act.wait_ge(free, jobs.filled("gate", HC - 1))
                nc.scalar.activation(tanh_gate[:], gate[:], ACT.Tanh, scale=0.5).then_inc(tanh_done, 1)

            def y_tanh(jobs, free):
                act.wait_ge(free, jobs.filled("down"))
                nc.scalar.activation(tanh_y[:], y[:], ACT.Tanh, scale=0.5).then_inc(tanh_done, 1)

            square(first_ws, main)
            square(second_ws, second)
            for jobs in ffn_jobs:
                gate_tanh(jobs, ffn_free)
                y_tanh(jobs, ffn_free)
            act.wait_ge(second.q_split, 1)

            def body(i, jobs, post, prep, first):
                for g in range(GROUPS):
                    if g == TANH_GATE_GROUP and prep:
                        gate_tanh(jobs, main.free)
                    if g == TANH_Y_GROUP and prep:
                        y_tanh(jobs, main.free)
                    act.wait_ge(scores_ready, i * GROUPS + g + 1)
                    if not first or g >= PRING:
                        act.wait_ge(probs_used, i * STEPS + (g - PRING) // 2 + 1)
                    nc.scalar.activation(probs[:, g % PRING, :, :], scores[:, slot_of(g), :, :], ACT.Exp,
                                         scale=SCORE_SCALE).then_inc(probs_ready, 1)

            run_bodies(act, body)

        @block.vector
        def _(dve):
            def rsqrt(x_, y_, t_, piece=None):
                if piece in (None, 0):
                    nc.vector.tensor_scalar(t_.bitcast(U32), x_.bitcast(U32), 1, None, ALU.logical_shift_right)
                    dve.drain()
                    last = nc.vector.tensor_scalar(y_.bitcast(I32), t_.bitcast(I32), -1.0, RSQRT_MAGIC,
                                                   ALU.mult, ALU.add)
                    dve.drain()
                for step in (1, 2, 3):
                    if piece in (None, step):
                        nc.vector.scalar_tensor_tensor(t_, y_, -0.5, y_, ALU.mult, ALU.mult)
                        dve.drain()
                        nc.vector.tensor_tensor(t_, t_, x_, ALU.mult)
                        dve.drain()
                        last = nc.vector.scalar_tensor_tensor(y_, t_, 1.5, y_, ALU.add, ALU.mult)
                        dve.drain()
                return last

            def x_stats(tiles):
                for t in tiles:
                    nc.vector.bn_stats(stats[:, t, :], x_all[:, t, :])
                dve.drain()
                for t in tiles:
                    nc.vector.bn_aggr(mv[:, t, :], stats[:, t, :])
                dve.drain()
                n = len(tiles)
                some = slice(tiles[0], tiles[0] + n)
                nc.vector.tensor_scalar(rs_x[:, 0, 0:n], mv[:, some, 1], LN_EPS, None, ALU.add)
                dve.drain()
                rsqrt(rs_x[:, 0, 0:n], ln_r[:, some], rs_t[:, 0, 0:n])

            def norm_x(u, ws, s):
                for t in range(T):
                    tile = bass.ds(u * T + t, 1)
                    last = nc.vector.tensor_scalar(ws.xn[:, t:t + 1, :], x_all[:, tile, :],
                                                   mv[:, tile, 0:1].rearrange("p a b -> p (a b)"), ln_r[:, tile],
                                                   ALU.subtract, ALU.mult)
                last.then_inc(s.xn_ready, 1)

            def sum_squares(p, ws, s):
                dve.wait_ge(s.sq_ready, p + 1)
                nc.vector.tensor_reduce(ws.rs_t, ws.sq.rearrange("p t (h d) -> p (t h) d", d=HD), AX_X, ALU.add)
                dve.drain()

            def rms(piece, p, s):
                x_, y_, t_ = rs_x[:, 0, :], rs_y[:, 0, :], rs_t[:, 0, :]
                if piece == 0:
                    sum_squares(p, first_ws, s)
                elif piece == 1:
                    nc.vector.tensor_scalar(x_, t_, 1.0 / HD, RMS_EPS, ALU.mult, ALU.add)
                    dve.drain()
                    rsqrt(x_, y_, t_, 0)
                else:
                    rsqrt(x_, y_, t_, piece - 1)
                    if piece == 4:
                        nc.vector.engine_nop().then_inc(s.rms_ready, 1)

            def split(m, ws, free, done):
                nc.vector.tensor_scalar(ws.full, ws.bank, norm_w[:, m:m + 1], None, ALU.mult).then_inc(free, 1)
                dve.drain()
                nc.vector.tensor_copy(ws.parts[:, m, 0, :], ws.full)
                dve.drain()
                nc.vector.tensor_tensor(ws.rest, ws.full, ws.parts[:, m, 0, :], ALU.subtract)
                dve.drain()
                nc.vector.tensor_copy(ws.parts[:, m, 1, :], ws.rest)
                dve.drain()
                nc.vector.tensor_tensor(ws.parts[:, m, 2, :], ws.rest, ws.parts[:, m, 1, :], ALU.subtract
                                        ).then_inc(done, 1)

            def prep_job(name, arg, u, p, jobs, ws, s):
                dve.wait_ge(s.filled, jobs.filled(name, arg))
                if name == "xT":
                    nc.vector.tensor_copy(ws.xT, ws.bank).then_inc(s.free, 1)
                elif name == "qkv":
                    nc.vector.tensor_tensor(ws.qk[:, arg, :], ws.bank[:, 0:2 * D], bqkv_b[:, 0:2 * D], ALU.add)
                    nc.vector.tensor_tensor(v_all[:, bass.ds(u * T + arg, 1), :],
                                            ws.bank[:, 2 * D:3 * D].unsqueeze(1),
                                            bqkv_b[:, 2 * D:3 * D].unsqueeze(1), ALU.add).then_inc(s.free, 1)
                elif name == "kT":
                    need(dve, s.k_stored, p * K_STORED)
                    split(arg, ws, s.free, s.k_split)
                else:
                    need(dve, s.q_stored, p * Q_STORED)
                    split(arg, ws, s.free, s.q_split)

            def ffn_job(name, arg, u, jobs, bank, free, filled):
                dve.wait_ge(filled, jobs.filled(name, arg))
                if name == "gate":
                    nc.vector.tensor_copy(gate[:, arg, :], bank).then_inc(free, 1)
                elif name == "up":
                    dve.wait_ge(tanh_done, u * 2 + 1)
                    nc.vector.scalar_tensor_tensor(tanh_gate[:, arg, :], tanh_gate[:, arg, :], 1.0, gate[:, arg, :],
                                                   ALU.add, ALU.mult)
                    dve.drain()
                    nc.vector.scalar_tensor_tensor(gate[:, arg, :], tanh_gate[:, arg, :], 0.5, bank,
                                                   ALU.mult, ALU.mult).then_inc(free, 1)
                else:
                    nc.vector.tensor_copy(y[:], bank).then_inc(free, 1)

            def gate_of_y(u):
                dve.wait_ge(tanh_done, u * 2 + 2)
                tiles = [t[:].rearrange("p (t c) -> p t c", t=T) for t in (tanh_y, y)]
                nc.vector.scalar_tensor_tensor(g2_all[:, bass.ds(u * T, T), :], tiles[0], 1.0, tiles[1],
                                               ALU.add, ALU.mult)
                dve.drain()

            def take_heads(q, i):
                dve.wait_ge(probs_used, i * STEPS + KT * (q + 1))
                nc.vector.tensor_copy(o_sb[:], heads_o[:]).then_inc(o_free, 1)

            def post_job(name, arg, i, jobs):
                dve.wait_ge(main.filled, jobs.filled(name, arg))
                if name == "heads":
                    sums = misc[:].rearrange("p (t j m) -> p t j m", t=T, m=VW)
                    nc.vector.reciprocal(denom_r[:], misc[:].rearrange("p (n m) -> p n m", m=VW)[:, :, HD])
                    dve.drain()
                    r = denom_r[:].rearrange("p (t j) -> p t j", t=T).unsqueeze(3).broadcast_to([P, T, 4, HD])
                    nc.vector.tensor_tensor(
                        attn[:, :, 4 * arg * HD:4 * (arg + 1) * HD].rearrange("p t (j d) -> p t j d", d=HD),
                        sums[:, :, :, 0:HD], r, ALU.mult).then_inc(main.free, 1)
                elif name == "attnT":
                    nc.vector.tensor_copy(attnT, misc[:]).then_inc(main.free, 1)
                else:
                    tiles = bass.ds((i - 1) * T, T)
                    joined_t = joined.rearrange("p (t c) -> p t c", t=T)
                    nc.vector.tensor_tensor(joined_t, misc[:].rearrange("p (t c) -> p t c", t=T),
                                            bproj_b[:].unsqueeze(1).broadcast_to([P, T, D]), ALU.add
                                            ).then_inc(main.free, 1)
                    dve.drain()
                    nc.vector.scalar_tensor_tensor(joined_t, joined_t, 0.5, g2_all[:, tiles, :], ALU.mult, ALU.mult)
                    dve.drain()
                    need(dve, out_stored, (i - 1) * 16)
                    nc.vector.tensor_tensor(joined_x[:], joined_t, x_all[:, tiles, :], ALU.add
                                            ).then_inc(out_ready, 1)

            nc.vector.memset(zeros, 0.0).then_inc(zeros_set, 1)
            dve.wait_ge(w_loaded, W_DMAS * 16)
            nc.vector.tensor_tensor(bound[0:1, 0:HD], norm_rows[0:1, 0, :], norm_rows[0:1, 1, :], ALU.mult)
            dve.drain()
            nc.vector.tensor_reduce(bound[0:1, HD:HD + 1], bound[0:1, 0:HD], AX_X, ALU.max,
                                    apply_absolute_value=True)
            dve.drain()
            nc.vector.tensor_scalar(bound[0:1, HD + 1:HD + 2], bound[0:1, HD:HD + 1],
                                    -1.0 if force_general else SAFE_BOUND / HD ** 0.5, None, ALU.is_le)
            dve.drain()
            nc.vector.tensor_scalar(unsafe[:], bound[0:1, HD + 1:HD + 2], -1.0, 1.0, ALU.mult, ALU.add
                                    ).then_inc(bound_ready, 1)

            def run_general():
                dve.wait_ge(x_first, 2 * 16)
                dve.wait_ge(x_rest, (UNITS - 2) * 16)
                x_stats(range(UNITS * T))
                with dve.Fori(0, UNITS) as u:
                    norm_x(u, first_ws, general)
                    jobs = Jobs(PREP_JOBS, u * N_PREP)
                    for name, arg in jobs.order:
                        prep_job(name, arg, u, u, jobs, first_ws, general)
                        if (name, arg) == ("qkv", T - 1):
                            for piece in range(5):
                                rms(piece, u, general)
                with dve.Fori(0, UNITS * H) as n:
                    for t in range(T):
                        dve.wait_ge(g_scores, n * T + t + 1)
                        nc.vector.tensor_reduce(row_max[:, t:t + 1], scores[:, t % 2, :, :], AX_XY, ALU.max
                                                ).then_inc(g_max, 1)
                    dve.drain()
                    dve.wait_ge(g_stored, n * (PARTS * 16))
                    nc.vector.tensor_scalar(shift_parts[:, 0, :], row_max[:], -1.0, None, ALU.mult)
                    dve.drain()
                    nc.vector.scalar_tensor_tensor(shift_rest[:], row_max[:], -1.0, shift_parts[:, 0, :],
                                                   ALU.mult, ALU.subtract)
                    dve.drain()
                    nc.vector.tensor_copy(shift_parts[:, 1, :], shift_rest[:])
                    dve.drain()
                    nc.vector.tensor_tensor(shift_parts[:, 2, :], shift_rest[:], shift_parts[:, 1, :],
                                            ALU.subtract).then_inc(g_shift, 1)
                dve.drain().then_inc(g_over, 1)

            general_path(dve, run_general)

            def both(name, arg):
                prep_job(name, arg, 0, 0, prep_jobs, first_ws, main)
                prep_job(name, arg, 1, 0, prep_jobs, second_ws, second)

            def early_ffn(unit, names):
                for name, arg in ffn_jobs[unit].order:
                    if name in names:
                        ffn_job(name, arg, unit, ffn_jobs[unit], ffn_bank, ffn_free, ffn_filled)

            dve.wait_ge(x_first, 2 * 16)
            x_stats(range(2 * T))
            norm_x(0, first_ws, main)
            norm_x(1, second_ws, second)
            both("xT", 0)
            for t in range(T):
                both("qkv", t)
            dve.wait_ge(ffn_loaded, FFN_DMAS * 16)
            nc.vector.tensor_scalar(w_ffn[:], w_int, W_SCALE, None, ALU.mult).then_inc(w_ready, 1)
            sum_squares(0, first_ws, main)
            sum_squares(0, second_ws, second)
            nc.vector.tensor_scalar(rs_x[:], rs_t[:], 1.0 / HD, RMS_EPS, ALU.mult, ALU.add)
            dve.drain()
            rsqrt(rs_x[:], rs_y[:], rs_t[:])
            nc.vector.engine_nop().then_inc(main.rms_ready, 1)
            nc.vector.engine_nop().then_inc(second.rms_ready, 1)
            early_ffn(0, ["gate"])
            both("kT", 1)
            both("qT", 0)
            early_ffn(0, ["up", "down"])
            gate_of_y(0)
            early_ffn(1, ["gate", "up", "down"])
            gate_of_y(1)
            dve.wait_ge(x_rest, (UNITS - 2) * 16)
            x_stats(range(2 * T, UNITS * T))

            def body(i, jobs, post, prep, first):
                for n in range(STEPS):
                    if n == 0 and prep:
                        norm_x(i + 2, first_ws, main)
                    if n == 0 and post:
                        take_heads(QUADS - 1, i - 1)
                    elif n and n % KT == 0:
                        take_heads(n // KT - 1, i)
                        if n == KT and first:
                            dve.wait_ge(second.k_stored, K_STORED)
                            dve.wait_ge(second.q_stored, Q_STORED)
                    for name, arg in jobs.at(n):
                        if (n, name, arg) in PREP_JOBS:
                            prep_job(name, arg, i + 2, i + 1, jobs, first_ws, main)
                        elif (n, name, arg) in FFN_JOBS:
                            ffn_job(name, arg, i + 2, jobs, misc_ap, main.free, main.filled)
                        else:
                            post_job(name, arg, i, jobs)
                    if n in RMS_STEPS and prep:
                        rms(RMS_STEPS[n], i + 1, main)
                if prep:
                    gate_of_y(i + 2)

            run_bodies(dve, body)
            take_heads(QUADS - 1, UNITS - 1)
            for name, arg in LAST_JOBS.order:
                post_job(name, arg, UNITS, LAST_JOBS)


def kernel(**inputs):
    import numpy as np
    import concourse.bacc as bacc
    from concourse.bass_utils import run_bass_kernel_spmd

    w_down = inputs["L0_ffn_w_down"]
    laid_out = {
        "x": inputs["L0_attn_x"],
        "WqkvT": inputs["L0_attn_Wqkv"].T,
        "bqkv": inputs["L0_attn_bqkv"],
        "WprojT": inputs["L0_attn_Wproj"].T,
        "bproj": inputs["L0_attn_bproj"],
        "qn_w": np.tile(np.asarray(inputs["L0_attn_qn_w"]), H)[None, :],
        "kn_w": np.tile(np.asarray(inputs["L0_attn_kn_w"]), H)[None, :],
        "w_gateT": inputs["L0_ffn_w_gate"].T,
        "w_upT": inputs["L0_ffn_w_up"].T,
        "w_downT": np.asarray(w_down).reshape(D, HC, P).transpose(2, 1, 0).reshape(P, HC * D),
    }
    nc = bacc.Bacc("TRN2", target_bir_lowering=False, num_devices=1)
    arrays, args = {}, []
    for name, a in laid_out.items():
        a = np.ascontiguousarray(a)
        arrays[f"in_{name}"] = a
        args.append(nc.dram_tensor(f"in_{name}", a.shape, mybir.dt.from_np(a.dtype), kind="ExternalInput").ap())
    out = nc.dram_tensor("out_0", (B, S, D), F32, kind="ExternalOutput").ap()
    attention_ffn(nc, *args, out)
    r = run_bass_kernel_spmd(nc, [arrays], core_ids=[0])
    return r.results[0]["out_0"]
```

```python
from contextlib import ExitStack

import concourse.bass as bass
from concourse import mybir

F32 = mybir.dt.float32
BF16 = mybir.dt.bfloat16
I32 = mybir.dt.int32
U32 = mybir.dt.uint32
ALU = mybir.AluOpType
ACT = mybir.ActivationFunctionType
AX_X = mybir.AxisListType.X
AX_XY = mybir.AxisListType.XY

P = 128
D = 128
H = 16
HD = D // H
HIDDEN = 384
HC = HIDDEN // P
B, S = 4, 1024
UNIT = 512
T = UNIT // P
UNITS = B * S // UNIT
QUADS = H // 4
KT = S // P
STEPS = QUADS * KT
GROUPS = 2 * STEPS
PARTS = 3
ROWS = PARTS * PARTS * HD
KROWS = ROWS + PARTS
SRING = 3
PRING = 8
VW = 32
BLOCKS = UNIT // VW
LN_EPS = 1e-5
RMS_EPS = 1e-6
W_SCALE = 1.0 / 127.0
SCORE_SCALE = HD ** -0.5
SAFE_BOUND = 60.0
RSQRT_MAGIC = 1597463007.0

POST_JOBS = [(2, "proj", 0)]
PREP_JOBS = [(7, "qkv", 0), (8, "qkv", 1), (9, "qkv", 2), (10, "qkv", 3)]
FFN_JOBS = [(4, "gate", 0), (5, "gate", 1), (6, "gate", 2), (12, "up", 0), (14, "up", 1), (16, "up", 2),
            (26, "down", 0)]
DOWN_STEPS = {20: 0, 22: 1, 24: 2, 26: 3}
X_T_STEP, K_T_STEP, K_SPLIT_STEP, Q_T_STEP, Q_SPLIT_STEP = 1, 17, 19, 21, 25
GENERAL_JOBS = [(0, "xT", 0)] + [(1 + t, "qkv", t) for t in range(T)] + [(5, "kT", 1), (6, "qT", 0)]
FIRST_JOBS = [(0, "xT", 0)] + [(1 + t, "qkv", t) for t in range(T)] + [(5, "qT", 0), (6, "kT", 1), (7, "down", 0), (8, "down", 1)]
SECOND_JOBS = GENERAL_JOBS
TANH_GATE_GROUP = 16
TANH_Y_GROUP = 60
LATE_TANH_GROUP = 8
LATE_G2_STEP = 6
X_STATS_STEPS = (26, 28, 29)
RMS_STEPS = {11: (0, 1), 12: (2,), 13: (3, 4)}


class Jobs:
    def __init__(self, jobs, before):
        self.order = [(name, arg) for _, name, arg in sorted(jobs)]
        self.steps = [step for step, _, _ in sorted(jobs)]
        self.before = before

    def free(self, name, arg=0):
        return self.before + self.order.index((name, arg))

    def filled(self, name, arg=0):
        return self.before + self.order.index((name, arg)) + 1

    def at(self, step):
        return [job for job, s in zip(self.order, self.steps) if s == step]


def jobs_of(post, prep, before):
    return Jobs(POST_JOBS * post + (PREP_JOBS + FFN_JOBS) * prep, before)


N_GENERAL, N_POST, N_FIRST = len(GENERAL_JOBS), len(POST_JOBS), len(FIRST_JOBS)
N_NEXT = len(PREP_JOBS) + len(FFN_JOBS)
LAST_JOBS = Jobs(POST_JOBS, N_FIRST + (UNITS - 2) * N_NEXT + (UNITS - 1) * N_POST)


def slot_of(g):
    return 1 if g == GROUPS - 1 else g % SRING


def last_user(g):
    slot = slot_of(g)
    return next(k for k in range(g - 1, g - 6, -1) if slot_of(k % GROUPS) == slot)


def attention_ffn(nc, x, WqkvT, bqkv, WprojT, bproj, qn_w, kn_w, w_gateT, w_upT, w_downT, out, force_general=False):
    with ExitStack() as ctx:
        def sb(name, shape, dt=F32):
            return ctx.enter_context(nc.sbuf_tensor(name, shape, dt))

        def sem(name):
            return ctx.enter_context(nc.semaphore(name))

        q_rows = nc.dram_tensor("q_rows", (UNITS, H, HD, PARTS, UNIT), BF16, kind="Internal").ap()
        k_rows = nc.dram_tensor("k_rows", (B, PARTS, HD, H, S), BF16, kind="Internal").ap()
        shifts = nc.dram_tensor("shifts", (UNITS, PARTS, H, UNIT), BF16, kind="Internal").ap()

        scores = ctx.enter_context(nc.psum_tensor("scores", [P, SRING, 2, 512], F32))
        heads_o = ctx.enter_context(nc.psum_tensor("heads_o", [P, UNIT], F32))
        misc = ctx.enter_context(nc.psum_tensor("misc", [P, 512], F32))

        x_all = sb("x_all", [P, UNITS * T, D])
        g2_all = sb("g2_all", [P, UNITS * T, D])
        v_all = sb("v_all", [P, UNITS * T, D])
        k_ring = sb("k_ring", [KROWS, QUADS, 4, S], BF16)
        q_ring = sb("q_ring", [KROWS, QUADS, 4, UNIT], BF16)
        v_ring = sb("v_ring", [P, QUADS, KT, 4, VW])
        probs = sb("probs", [P, PRING, 2, UNIT])
        ident = sb("ident", [P, P])
        wqkv = sb("wqkv", [P, 3 * D])
        bqkv_b = sb("bqkv_b", [P, 3 * D])
        wproj = sb("wproj", [P, D])
        bproj_b = sb("bproj_b", [P, D])
        norm_w = sb("norm_w", [P, 2])
        norm_rows = sb("norm_rows", [1, 2, HD])
        bound = sb("bound", [1, HD + 2])
        unsafe = sb("unsafe", [1, 1], I32)
        w_ffn = sb("w_ffn", [P, 3, HIDDEN])
        early = probs[:].rearrange("p a b c -> p (a b c)")
        w_int = early[:, 0:3 * HIDDEN].bitcast(I32).rearrange("p (w h) -> p w h", w=3)
        zero_words = UNITS * PARTS * H * UNIT // P // 2
        zeros = early[:, 3 * HIDDEN:3 * HIDDEN + zero_words]
        early_at = [3 * HIDDEN + zero_words]
        stats = sb("stats", [P, UNITS * T, 6])
        mv = sb("mv", [P, UNITS * T, 2])
        ln_r = sb("ln_r", [P, UNITS * T])
        rs_x = sb("rs_x", [P, 2, P])
        rs_y = sb("rs_y", [P, 2, P])
        rs_t = sb("rs_t", [P, 2, P])

        def early_room(name, shape, dt=F32):
            words = 1
            for n in shape[1:]:
                words *= n
            words = words * (2 if dt is BF16 else 4) // 4
            at = early_at[0]
            early_at[0] += words
            flat = early[:, at:at + words]
            flat = flat.bitcast(BF16) if dt is BF16 else flat
            if len(shape) == 3:
                return flat.rearrange("p (a b) -> p a b", a=shape[1])
            if len(shape) == 4:
                return flat.rearrange("p (a b c) -> p a b c", a=shape[1], b=shape[2])
            return flat

        class Workspace:
            def __init__(self, tag, room, bank, n, parts=None):
                self.bank = bank
                self.xn = room(tag + "xn", [P, T, D])
                self.xT = room(tag + "xT", [P, UNIT])
                self.qk = room(tag + "qk", [P, T, 2 * D])
                self.sq = room(tag + "sq", [P, T, 2 * D])
                self.qkn = self.sq
                self.full = room(tag + "full", [P, UNIT])
                self.rest = room(tag + "rest", [P, UNIT])
                self.parts = room(tag + "parts", [P, 2, PARTS, UNIT], BF16) if parts is None else parts
                self.rs_t, self.rs_y = rs_t[:, n, :], rs_y[:, n, :]
        gate = sb("gate", [P, HC, UNIT])
        tanh_gate = sb("tanh_gate", [P, HC, UNIT])
        y = sb("y", [P, UNIT])
        tanh_y = sb("tanh_y", [P, UNIT])
        heads_t = sb("heads_t", [P, BLOCKS, VW])
        denom_r = sb("denom_r", [P, BLOCKS])
        post_room = sb("post_room", [P, 3, UNIT])
        attn = post_room[:, 0, :].rearrange("p (b c) -> p b c", b=BLOCKS)
        attnT, joined = post_room[:, 1, :], post_room[:, 2, :]
        second_parts = post_room[:].rearrange("p a b -> p (a b)").bitcast(BF16).rearrange(
            "p (m c s) -> p m c s", m=2, c=PARTS)
        joined_x = sb("joined_x", [P, T, D])
        row_max = sb("row_max", [P, T])
        shift_rest = sb("shift_rest", [P, T])
        shift_parts = sb("shift_parts", [P, PARTS, T], BF16)

        class Sems:
            def __init__(self, tag, early=0):
                self.early = early
                self.filled = sem(tag + "filled")
                self.free = sem(tag + "free")
                self.xn_ready = sem(tag + "xn_ready")
                self.sq_ready = sem(tag + "sq_ready")
                self.rms_ready = sem(tag + "rms_ready")
                self.qkn_ready = sem(tag + "qkn_ready")
                self.k_second = sem(tag + "k_second")
                self.k_split = sem(tag + "k_split")
                self.q_split = sem(tag + "q_split")
                self.k_stored = sem(tag + "k_stored")
                self.q_stored = sem(tag + "q_stored")

        def tile(name, shape, dt=F32):
            return sb(name, shape, dt)[:]

        misc_ap = misc[:]
        first_ws = Workspace("a_", tile, misc_ap, 0)
        second_ws = Workspace("b_", early_room, scores[:, 0, 0, :], 1, second_parts)
        assert early_at[0] <= PRING * 2 * UNIT
        banks = scores[:].rearrange("p a b c -> p (a b) c")
        gate_banks = banks[:, 1:1 + HC, :]
        up_banks = [banks[:, 4, :], banks[:, 5, :], heads_o[:]]
        main = Sems("")
        second = Sems("b_")
        general = Sems("g_", early=1)
        ffn_filled = sem("ffn_filled")
        ffn_free = sem("ffn_free")
        xT_ready = sem("xT_ready")
        full_ready = sem("full_ready")
        part_ready = sem("part_ready")
        attn_ready = sem("attn_ready")
        norm_loaded = sem("norm_loaded")
        w_loaded = sem("w_loaded")
        ffn_loaded = sem("ffn_loaded")
        x_first = sem("x_first")
        x_rest = sem("x_rest")
        ident_zero = sem("ident_zero")
        ident_ready = sem("ident_ready")
        ring_set = sem("ring_set")
        ones_set = sem("ones_set")
        zeros_set = sem("zeros_set")
        w_ready = sem("w_ready")
        bound_ready = sem("bound_ready")
        shifts_zero = sem("shifts_zero")
        kq_loaded = [sem(f"kq_loaded{q}") for q in range(QUADS)]
        v_loaded = [sem(f"v_loaded{q}") for q in range(QUADS)]
        v_turns = sem("v_turns")
        scores_ready = sem("scores_ready")
        probs_ready = sem("probs_ready")
        probs_used = sem("probs_used")
        o_free = sem("o_free")
        gate_tanh_done = sem("gate_tanh_done")
        y_tanh_done = sem("y_tanh_done")
        out_ready = sem("out_ready")
        out_stored = sem("out_stored")
        g_loaded = sem("g_loaded")
        g_scores = sem("g_scores")
        g_max = sem("g_max")
        g_shift = sem("g_shift")
        g_stored = sem("g_stored")
        g_over = sem("g_over")

        K_STORED = PARTS * 16
        Q_STORED = 16
        W_DMAS = 4
        FFN_DMAS = 5
        HEAD_DMAS = 2 * PARTS
        KQ_DMAS = 2 * PARTS + 1
        ENGINES = 5

        x_v = x.rearrange("b (t p) c -> p (b t) c", p=P)
        out_v = out.rearrange("b (u t p) c -> (b u) p t c", p=P, t=T)

        def need(engine, semaphore, value):
            if not isinstance(value, int) or value > 0:
                engine.wait_ge(semaphore, value)

        block = ctx.enter_context(nc.Block())

        def run_bodies(engine, body):
            before = N_FIRST
            body(0, jobs_of(0, 1, before), post=False, prep=True, first=True)
            before += N_NEXT
            step = N_NEXT + N_POST
            with engine.Fori(0, UNITS - 3) as k:
                body(k + 1, jobs_of(1, 1, k * step + before), post=True, prep=True, first=False)
            before += (UNITS - 3) * step
            with engine.Fori(0, 2) as k:
                body(k + UNITS - 2, jobs_of(1, 0, k * N_POST + before), post=True, prep=False, first=False)

        first_jobs, second_jobs = Jobs(FIRST_JOBS, 0), Jobs(SECOND_JOBS, 0)

        def general_path(engine, run):
            engine.wait_ge(bound_ready, 1)
            flag = engine.value_load(unsafe[0:1, 0:1], min_val=0, max_val=1)
            with engine.If(flag > 0):
                run()
                engine.wait_ge(g_over, ENGINES)

        @block.sync
        def _(sp):
            for u in range(UNITS):
                sp.dma_start(x_all[:, u * T:(u + 1) * T, :], x_v[:, u * T:(u + 1) * T, :]).then_inc(
                    x_first if u < 2 else x_rest, 16)
            sp.sem_inc(out_stored, 16)
            sp.wait_ge(zeros_set, 1)
            sp.dma_start(shifts.rearrange("u a h s -> (u a h s)").rearrange("(p f) -> p f", p=P),
                         zeros.bitcast(BF16)).then_inc(shifts_zero, 16)

            def store_k_part(c, u, ws, s):
                dst = k_rows[bass.ds(u // 2, 1), c, :, :, bass.ds(u % 2 * UNIT, UNIT)]
                sp.dma_start(dst.rearrange("b d h s -> h d (b s)"), ws.parts[:, 1, c, :]).then_inc(s.k_stored, 16)

            def store_k(u, p, ws, s):
                sp.wait_ge(s.k_split, p + 1)
                for c in range(PARTS):
                    store_k_part(c, u, ws, s)

            def store_q(u, p, ws, s):
                sp.wait_ge(s.q_split, p + 1)
                sp.dma_start(q_rows[bass.ds(u, 1)].rearrange("u h d r s -> (u h d) r s"), ws.parts[:, 0, :, :]
                             ).then_inc(s.q_stored, 16)

            def load_q(i, heads, slot, n, done):
                src = q_rows[bass.ds(i, 1), heads, :, :, :].rearrange("u h d r s -> (u d r) h s")
                for c in range(PARTS):
                    sp.dma_start(q_ring[c * PARTS * HD:(c + 1) * PARTS * HD, slot, 0:n, :], src).then_inc(done, 16)

            def load_k(i, heads, slot, n, done):
                src = k_rows[bass.ds(i // 2, 1), :, :, heads, :].rearrange("b c d h s -> (b c d) h s")
                for r in range(PARTS):
                    sp.dma_start(k_ring[r:ROWS:PARTS, slot, 0:n, :], src).then_inc(done, 16)

            def load_shifts(i, q, done):
                sp.dma_start(q_ring[ROWS:KROWS, q, :, :], shifts[bass.ds(i, 1), :, 4 * q:4 * q + 4, :].rearrange(
                    "u a h s -> (u a) h s")).then_inc(done, 16)

            def load_quads(i, quads, first=False):
                for q in quads:
                    if not first:
                        sp.wait_ge(probs_used, (i - 1) * STEPS + KT * (q + 1))
                    heads = slice(4 * q, 4 * q + 4)
                    load_k(i, heads, q, 4, kq_loaded[q])
                    load_q(i, heads, q, 4, kq_loaded[q])
                    load_shifts(i, q, kq_loaded[q])

            def store_out(i):
                sp.wait_ge(out_ready, i + 1)
                sp.dma_start(out_v[bass.ds(i, 1)].rearrange("a p t c -> p (a t) c"), joined_x[:]).then_inc(out_stored, 16)

            sp.wait_ge(shifts_zero, 16)

            def run_general():
                sp.sem_inc(general.k_stored, K_STORED)
                sp.sem_inc(general.q_stored, Q_STORED)
                sp.sem_inc(g_stored, PARTS * 16)
                with sp.Fori(0, UNITS) as u:
                    store_k(u, u, first_ws, general)
                    store_q(u, u, first_ws, general)
                sp.wait_ge(general.k_stored, (UNITS + 1) * K_STORED)
                sp.wait_ge(general.q_stored, (UNITS + 1) * Q_STORED)
                with sp.Fori(0, UNITS) as u:
                    with sp.Fori(0, H) as h:
                        n = u * H + h
                        load_k(u, bass.ds(h, 1), 0, 1, g_loaded)
                        load_q(u, bass.ds(h, 1), 0, 1, g_loaded)
                        sp.wait_ge(g_shift, n + 2)
                        dst = shifts[bass.ds(u, 1), :, bass.ds(h, 1), :].rearrange("u a h (t p) -> p (u a h) t", p=P)
                        for a in range(PARTS):
                            sp.dma_start(dst[:, a, :], shift_parts[:, a, :], allow_slow_non_contiguous=True
                                         ).then_inc(g_stored, 16)
                sp.wait_ge(g_stored, (UNITS * H + 1) * PARTS * 16)
                sp.drain().then_inc(g_over, 1)

            general_path(sp, run_general)

            sp.wait_ge(part_ready, 2)
            store_k_part(0, 1, second_ws, second)
            store_q(0, 0, first_ws, main)
            sp.wait_ge(part_ready, 3)
            store_k_part(0, 0, first_ws, main)
            sp.wait_ge(second.k_second, 1)
            store_k_part(1, 1, second_ws, second)
            sp.wait_ge(second.k_split, 1)
            store_k_part(2, 1, second_ws, second)
            sp.wait_ge(main.k_second, 1)
            store_k_part(1, 0, first_ws, main)
            sp.wait_ge(main.k_split, 1)
            store_k_part(2, 0, first_ws, main)
            sp.wait_ge(ones_set, 1)
            sp.wait_ge(main.q_stored, Q_STORED)
            load_q(0, slice(0, 4), 0, 4, kq_loaded[0])
            load_shifts(0, 0, kq_loaded[0])
            sp.wait_ge(second.k_stored, K_STORED)
            sp.wait_ge(main.k_stored, K_STORED)
            load_k(0, slice(0, 4), 0, 4, kq_loaded[0])
            load_quads(0, range(1, QUADS), first=True)
            store_q(1, 0, second_ws, second)

            def body(i, jobs, post, prep, first):
                if not first:
                    sp.wait_ge(main.k_stored, (i + 1) * K_STORED if prep else (UNITS - 1) * K_STORED)
                    sp.wait_ge(main.q_stored, i * Q_STORED)
                    load_quads(i, range(QUADS))
                if post:
                    store_out(i - 1)
                if prep:
                    store_k(i + 2, i + 1, first_ws, main)
                    store_q(i + 2, i + 1, first_ws, main)
                if first:
                    sp.wait_ge(second.q_stored, Q_STORED)

            run_bodies(sp, body)
            store_out(UNITS - 1)
            sp.wait_ge(out_stored, (UNITS + 1) * 16)
            sp.wait_ge(main.k_stored, (UNITS - 1) * K_STORED)
            sp.wait_ge(main.q_stored, (UNITS - 1) * Q_STORED)

        @block.gpsimd
        def _(pool):
            nc.gpsimd.memset(ident[:], 0.0).then_inc(ident_zero, 1)
            pool.wait_ge(ident_zero, 1)
            nc.gpsimd.affine_select(out=ident[:], in_=ident[:], compare_op=ALU.not_equal, fill=1.0, base=0,
                                    pattern=[[-1, P]], channel_multiplier=1).then_inc(ident_ready, 1)

            pool.wait_ge(ident_ready, 1)
            nc.gpsimd.memset(k_ring[64:KROWS, :, :, :].bitcast(U32), 0x3F803F80).then_inc(ring_set, 1)
            pool.wait_ge(ring_set, 1)
            nc.gpsimd.memset(v_ring[:], 0.0).then_inc(ring_set, 1)
            pool.wait_ge(ring_set, 2)
            nc.gpsimd.memset(v_ring[:, :, :, :, HD:HD + 1], 1.0).then_inc(ones_set, 1)
            pool.wait_ge(ffn_loaded, FFN_DMAS * 16)
            nc.gpsimd.tensor_scalar(w_ffn[:], w_int, W_SCALE, None, ALU.mult).then_inc(w_ready, 1)

            def square(jobs, ws, s):
                pool.wait_ge(s.free, jobs.filled("qkv", T - 1) + s.early)
                nc.gpsimd.tensor_tensor(ws.sq, ws.qk, ws.qk, ALU.mult).then_inc(s.sq_ready, 1)

            def norm(m, p, ws, s):
                pool.wait_ge(s.rms_ready, p + 1)
                some = slice(m * D, (m + 1) * D)
                heads = ws.qk[:, :, some].rearrange("p t (h d) -> p t h d", d=HD)
                r = ws.rs_y.rearrange("p (t h) -> p t h", t=T)[:, :, m * H:(m + 1) * H]
                nc.gpsimd.tensor_tensor(ws.qkn[:, :, some].rearrange("p t (h d) -> p t h d", d=HD), heads,
                                        r.unsqueeze(3).broadcast_to(heads.shape), ALU.mult).then_inc(s.qkn_ready, 1)

            def other_parts(n, m, ws, done):
                pool.wait_ge(part_ready, n + 1)
                nc.gpsimd.tensor_tensor(ws.rest, ws.full, ws.parts[:, m, 0, :], ALU.subtract)
                pool.drain()
                second_part = nc.gpsimd.tensor_copy(ws.parts[:, m, 1, :], ws.rest)
                if m == 1:
                    second_part.then_inc(second.k_second, 1)
                pool.drain()
                nc.gpsimd.tensor_tensor(ws.parts[:, m, 2, :], ws.rest, ws.parts[:, m, 1, :], ALU.subtract
                                        ).then_inc(done, 1)

            def load_v(i, first):
                for q in range(QUADS):
                    if not first:
                        pool.wait_ge(probs_used, (i - 1) * STEPS + KT * (q + 1))
                        pool.sem_inc(v_turns, 1)
                    for t in range(KT):
                        src = v_all[:, bass.ds(i // 2 * KT + t, 1), 4 * q * HD:4 * (q + 1) * HD]
                        move = nc.gpsimd.tensor_copy(v_ring[:, q, t, :, 0:HD],
                                                     src.rearrange("p t (h d) -> p (t h) d", d=HD))
                    move.then_inc(v_loaded[q], 1)

            def run_general():
                with pool.Fori(0, UNITS) as u:
                    square(Jobs(GENERAL_JOBS, u * N_GENERAL), first_ws, general)
                    norm(1, u, first_ws, general)
                    norm(0, u, first_ws, general)
                pool.drain().then_inc(g_over, 1)

            general_path(pool, run_general)

            pool.wait_ge(ones_set, 1)
            pool.wait_ge(main.free, first_jobs.filled("qkv", T - 1))
            pool.wait_ge(second.free, second_jobs.filled("qkv", T - 1))
            load_v(0, first=True)
            norm(0, 0, first_ws, main)
            norm(1, 0, second_ws, second)
            norm(1, 0, first_ws, main)
            norm(0, 0, second_ws, second)
            other_parts(1, 1, second_ws, second.k_split)
            other_parts(3, 0, second_ws, second.q_split)

            def body(i, jobs, post, prep, first):
                if not first:
                    load_v(i, first)
                if prep:
                    square(jobs, first_ws, main)
                    norm(1, i + 1, first_ws, main)
                    norm(0, i + 1, first_ws, main)

            run_bodies(pool, body)

        @block.tensor
        def _(pe):
            def transposed(bank, tiles):
                for t, tile in enumerate(tiles):
                    last = nc.tensor.transpose(bank[:, t * P:(t + 1) * P], tile, ident[:])
                return last

            def prep_job(name, arg, p, jobs, ws, s):
                halves = [job for job, _ in jobs.order if job in ("kT", "qT")]
                need(pe, s.free, jobs.free(name, arg) + s.early)
                if name == "xT":
                    pe.wait_ge(s.xn_ready, p + 1)
                    last = transposed(ws.bank, [ws.xn[:, t, :] for t in range(T)])
                elif name == "qkv":
                    last = nc.tensor.matmul(ws.bank[:, 0:3 * D], ws.xT[:, arg * P:(arg + 1) * P], wqkv[:],
                                            start=True, stop=True)
                else:
                    pe.wait_ge(s.qkn_ready, 2 * p + 1 + halves.index(name))
                    last = transposed(ws.bank, [ws.qkn[:, t, arg * D:(arg + 1) * D] for t in range(T)])
                last.then_inc(s.filled, 1)

            def ffn_job(name, arg, i, jobs):
                need(pe, main.free, jobs.free(name, arg))
                if (name, arg) == ("gate", 0):
                    pe.wait_ge(xT_ready, i + 1)
                w = w_ffn[:, 0 if name == "gate" else 1, arg * P:(arg + 1) * P]
                nc.tensor.matmul(misc_ap, w, first_ws.xT, start=True, stop=True).then_inc(main.filled, 1)

            def down(tiles, jobs, arg=0):
                if tiles[0] == 0:
                    pe.wait_ge(main.free, jobs.free("down", arg))
                for t in tiles:
                    for c in range(HC):
                        last = nc.tensor.matmul(misc[:, t * D:(t + 1) * D], gate[:, c, t * P:(t + 1) * P],
                                                w_ffn[:, 2, c * D:(c + 1) * D], start=c == 0, stop=c == HC - 1)
                if tiles[-1] == T - 1:
                    last.then_inc(main.filled, 1)

            def project(i, jobs):
                need(pe, main.free, jobs.free("proj"))
                pe.wait_ge(attn_ready, i)
                for t in range(T):
                    last = nc.tensor.matmul(misc[:, t * D:(t + 1) * D], attnT[:, t * P:(t + 1) * P], wproj[:],
                                            start=True, stop=True)
                last.then_inc(main.filled, 1)

            pe.wait_ge(ident_ready, 1)
            pe.wait_ge(w_loaded, W_DMAS * 16)

            def run_general():
                with pe.Fori(0, UNITS) as u:
                    jobs = Jobs(GENERAL_JOBS, u * N_GENERAL)
                    for name, arg in jobs.order:
                        prep_job(name, arg, u, jobs, first_ws, general)
                with pe.Fori(0, UNITS * H) as n:
                    pe.wait_ge(g_loaded, (n + 1) * (HEAD_DMAS * 16))
                    for t in range(T):
                        if t < 2:
                            pe.wait_ge(g_shift, n + 1)
                        else:
                            pe.wait_ge(g_max, n * T + t - 1)
                        for half in range(2):
                            last = nc.tensor.matmul(scores[:, t % 2, half, :], q_ring[0:ROWS, 0, 0, t * P:(t + 1) * P],
                                                    k_ring[0:ROWS, 0, 0, half * 512:(half + 1) * 512],
                                                    start=True, stop=True)
                        last.then_inc(g_scores, 1)
                pe.drain().then_inc(g_over, 1)

            general_path(pe, run_general)

            def first_job(name, arg):
                prep_job(name, arg, 0, first_jobs, first_ws, main)

            def second_job(name, arg):
                prep_job(name, arg, 0, second_jobs, second_ws, second)

            def early_hidden(unit, which, banks):
                for c in range(HC):
                    last = nc.tensor.matmul(banks[c], w_ffn[:, which, c * P:(c + 1) * P],
                                            (first_ws, second_ws)[unit].xT, start=True, stop=True)
                last.then_inc(ffn_filled, 1)

            def keep_warm(n, bank):
                for _ in range(n):
                    nc.tensor.matmul(bank[:, 0:3 * D], ident[:], wqkv[:], start=True, stop=True)

            gates = [gate_banks[:, c, :] for c in range(HC)]
            first_job("xT", 0)
            second_job("xT", 0)
            for t in range(T):
                first_job("qkv", t)
                second_job("qkv", t)
            pe.wait_ge(w_ready, 1)
            early_hidden(0, 0, gates)
            early_hidden(0, 1, up_banks)
            pe.wait_ge(main.free, first_jobs.free("qT"))
            keep_warm(7, misc_ap)
            first_job("qT", 0)
            second_job("kT", 1)
            first_job("kT", 1)
            pe.wait_ge(ffn_free, 1)
            early_hidden(1, 0, gates)
            second_job("qT", 0)
            pe.wait_ge(ffn_free, 2)
            down(range(T), first_jobs)
            early_hidden(1, 1, up_banks)
            pe.wait_ge(ffn_free, 3)
            keep_warm(3, gates[0])
            pe.wait_ge(ffn_free, 4)
            down([0, 1], first_jobs, 1)

            def score_group(g, i, first):
                q, t, pair = g // (2 * KT), g // 2 % KT, g % 2
                if first and g == 0:
                    pe.wait_ge(second.free, N_GENERAL)
                if g % (2 * KT) == 0:
                    pe.wait_ge(kq_loaded[q], (i + 1) * (KQ_DMAS * 16))
                if not first or last_user(g) >= 0:
                    pe.wait_ge(probs_ready, i * GROUPS + last_user(g) + 1)
                for k in range(2):
                    j = 2 * pair + k
                    last = nc.tensor.matmul(scores[:, slot_of(g), k, :], k_ring[:, q, j, t * P:(t + 1) * P],
                                            q_ring[:, q, j, :], start=True, stop=True)
                last.then_inc(scores_ready, 1)

            def weigh_v(n, i):
                q, t = n // KT, n % KT
                if t == 0:
                    pe.wait_ge(v_loaded[q], i + 1)
                    need(pe, o_free, i * QUADS + q)
                pe.wait_ge(probs_ready, i * GROUPS + 2 * n + 2)
                for j in range(4):
                    last = nc.tensor.matmul(heads_o[j * VW:(j + 1) * VW, :], v_ring[:, q, t, j, :],
                                            probs[:, (2 * n + j // 2) % PRING, j % 2, :],
                                            start=t == 0, stop=t == KT - 1)
                last.then_inc(probs_used, 1)

            def body(i, jobs, post, prep, first):
                score_group(0, i, first)
                for n in range(STEPS):
                    score_group(2 * n + 1, i, first)
                    if not prep and n < STEPS - 1:
                        score_group(2 * n + 2, i, first)
                    if n > 0:
                        weigh_v(n - 1, i)
                    elif post:
                        weigh_v(STEPS - 1, i - 1)
                    if prep and n < STEPS - 1:
                        score_group(2 * n + 2, i, first)
                    for name, arg in jobs.at(n):
                        if (n, name, arg) in PREP_JOBS:
                            prep_job(name, arg, i + 1, jobs, first_ws, main)
                        elif name == "proj":
                            project(i, jobs)
                        elif name != "down":
                            ffn_job(name, arg, i, jobs)
                    if prep and n in DOWN_STEPS:
                        down([DOWN_STEPS[n]], jobs)
                    if first and n < 2:
                        down([2 + n], first_jobs, 1)

            run_bodies(pe, body)
            weigh_v(STEPS - 1, UNITS - 1)
            project(UNITS, LAST_JOBS)

        @block.scalar
        def _(act):
            act.dma_start(norm_rows[0:1, 0, :], qn_w[0:1, 0:HD]).then_inc(norm_loaded, 16)
            act.dma_start(norm_rows[0:1, 1, :], kn_w[0:1, 0:HD]).then_inc(norm_loaded, 16)
            act.dma_start(wqkv[:], WqkvT).then_inc(w_loaded, 16)
            act.dma_start(bqkv_b[:], bqkv.partition_broadcast(P)).then_inc(w_loaded, 16)
            act.dma_start(norm_w[:, 0:1], qn_w.rearrange("a p -> p a")).then_inc(w_loaded, 16)
            act.dma_start(norm_w[:, 1:2], kn_w.rearrange("a p -> p a")).then_inc(w_loaded, 16)
            act.dma_start(w_int[:, 0, :], w_gateT).then_inc(ffn_loaded, 16)
            act.dma_start(w_int[:, 1, :], w_upT).then_inc(ffn_loaded, 16)
            act.dma_start(w_int[:, 2, :], w_downT).then_inc(ffn_loaded, 16)
            act.dma_start(wproj[:], WprojT).then_inc(ffn_loaded, 16)
            act.dma_start(bproj_b[:], bproj.partition_broadcast(P)).then_inc(ffn_loaded, 16)

            def run_general():
                act.drain().then_inc(g_over, 1)

            general_path(act, run_general)

            def square(jobs, ws, s):
                act.wait_ge(s.free, jobs.filled("qkv", T - 1))
                nc.scalar.activation(ws.sq, ws.qk, ACT.Square).then_inc(s.sq_ready, 1)

            def early_gate_tanh(unit):
                act.wait_ge(ffn_filled, 2 * unit + 1)
                need(act, ffn_free, 2 * unit)
                nc.scalar.activation(tanh_gate[:], gate_banks, ACT.Tanh, scale=0.5).then_inc(gate_tanh_done, 1)

            def gate_tanh(jobs):
                act.wait_ge(main.free, jobs.filled("gate", HC - 1))
                nc.scalar.activation(tanh_gate[:], gate[:], ACT.Tanh, scale=0.5).then_inc(gate_tanh_done, 1)

            def y_tanh(jobs, arg=0):
                act.wait_ge(main.free, jobs.filled("down", arg))
                nc.scalar.activation(tanh_y[:], y[:], ACT.Tanh, scale=0.5).then_inc(y_tanh_done, 1)

            def first_part(n, m, ws):
                act.wait_ge(full_ready, n + 1)
                nc.scalar.activation(ws.parts[:, m, 0, :], ws.full, ACT.Copy).then_inc(part_ready, 1)

            square(first_jobs, first_ws, main)
            square(second_jobs, second_ws, second)
            early_gate_tanh(0)
            for n, (m, ws) in enumerate(((0, first_ws), (1, second_ws), (1, first_ws), (0, second_ws))):
                if n == 3:
                    early_gate_tanh(1)
                first_part(n, m, ws)
            y_tanh(first_jobs)
            act.wait_ge(second.q_split, 1)

            def body(i, jobs, post, prep, first):
                for g in range(GROUPS):
                    if g == TANH_GATE_GROUP and prep:
                        gate_tanh(jobs)
                    if g == LATE_TANH_GROUP and first:
                        y_tanh(first_jobs, 1)
                    if g == TANH_Y_GROUP and prep:
                        y_tanh(jobs)
                    act.wait_ge(scores_ready, i * GROUPS + g + 1)
                    if not first or g >= PRING:
                        act.wait_ge(probs_used, i * STEPS + (g - PRING) // 2 + 1)
                    nc.scalar.activation(probs[:, g % PRING, :, :], scores[:, slot_of(g), :, :], ACT.Exp,
                                         scale=SCORE_SCALE).then_inc(probs_ready, 1)

            run_bodies(act, body)

        @block.vector
        def _(dve):
            def rsqrt(x_, y_, t_, piece=None):
                if piece in (None, 0):
                    nc.vector.tensor_scalar(t_.bitcast(U32), x_.bitcast(U32), 1, None, ALU.logical_shift_right)
                    dve.drain()
                    last = nc.vector.tensor_scalar(y_.bitcast(I32), t_.bitcast(I32), -1.0, RSQRT_MAGIC,
                                                   ALU.mult, ALU.add)
                    dve.drain()
                for step in (1, 2, 3):
                    if piece in (None, step):
                        nc.vector.scalar_tensor_tensor(t_, y_, -0.5, y_, ALU.mult, ALU.mult)
                        dve.drain()
                        nc.vector.tensor_tensor(t_, t_, x_, ALU.mult)
                        dve.drain()
                        last = nc.vector.scalar_tensor_tensor(y_, t_, 1.5, y_, ALU.add, ALU.mult)
                        dve.drain()
                return last

            def x_sums(tiles):
                for t in tiles:
                    nc.vector.bn_stats(stats[:, t, :], x_all[:, t, :])
                dve.drain()
                for t in tiles:
                    nc.vector.bn_aggr(mv[:, t, :], stats[:, t, :])
                dve.drain()

            def x_rsqrt(tiles):
                n = len(tiles)
                some = slice(tiles[0], tiles[0] + n)
                nc.vector.tensor_scalar(rs_x[:, 0, 0:n], mv[:, some, 1], LN_EPS, None, ALU.add)
                dve.drain()
                rsqrt(rs_x[:, 0, 0:n], ln_r[:, some], rs_t[:, 0, 0:n])

            def norm_x(u, ws, s):
                for t in range(T):
                    tile = bass.ds(u * T + t, 1)
                    last = nc.vector.tensor_scalar(ws.xn[:, t:t + 1, :], x_all[:, tile, :],
                                                   mv[:, tile, 0:1].rearrange("p a b -> p (a b)"), ln_r[:, tile],
                                                   ALU.subtract, ALU.mult)
                last.then_inc(s.xn_ready, 1)

            def sum_squares(p, ws, s):
                dve.wait_ge(s.sq_ready, p + 1)
                nc.vector.tensor_reduce(ws.rs_t, ws.sq.rearrange("p t (h d) -> p (t h) d", d=HD), AX_X, ALU.add)
                dve.drain()

            def rms(piece, p, s):
                x_, y_, t_ = rs_x[:, 0, :], rs_y[:, 0, :], rs_t[:, 0, :]
                if piece == 0:
                    sum_squares(p, first_ws, s)
                elif piece == 1:
                    nc.vector.tensor_scalar(x_, t_, 1.0 / HD, RMS_EPS, ALU.mult, ALU.add)
                    dve.drain()
                    rsqrt(x_, y_, t_, 0)
                else:
                    rsqrt(x_, y_, t_, piece - 1)
                    if piece == 4:
                        nc.vector.engine_nop().then_inc(s.rms_ready, 1)

            def transposed(out, tiles):
                for a in range(0, P, VW):
                    for b in range(0, P, VW):
                        nc.vector.transpose(out.rearrange("p (t s) -> p t s", t=T)[b:b + VW, :, a:a + VW],
                                            tiles[a:a + VW, :, b:b + VW])

            def transposed_x():
                transposed(first_ws.xT, first_ws.xn)
                dve.drain().then_inc(xT_ready, 1)

            def transposed_qk(m, p):
                dve.wait_ge(main.qkn_ready, 2 * p + 2 - m)
                transposed(first_ws.rest, first_ws.qkn[:, :, m * D:(m + 1) * D])
                dve.drain()

            def split_transposed(m, stored, count, done):
                ws = first_ws
                nc.vector.tensor_scalar(ws.full, ws.rest, norm_w[:, m:m + 1], None, ALU.mult)
                dve.drain()
                dve.wait_ge(stored, count)
                nc.vector.tensor_copy(ws.parts[:, m, 0, :], ws.full)
                dve.drain()
                other_parts(m, ws).then_inc(done, 1)
                dve.drain()

            def weighted(m, ws):
                return nc.vector.tensor_scalar(ws.full, ws.bank, norm_w[:, m:m + 1], None, ALU.mult)

            def other_parts(m, ws, early_k=False):
                nc.vector.tensor_tensor(ws.rest, ws.full, ws.parts[:, m, 0, :], ALU.subtract)
                dve.drain()
                second_part = nc.vector.tensor_copy(ws.parts[:, m, 1, :], ws.rest)
                if early_k:
                    second_part.then_inc(main.k_second, 1)
                dve.drain()
                return nc.vector.tensor_tensor(ws.parts[:, m, 2, :], ws.rest, ws.parts[:, m, 1, :], ALU.subtract)

            def split(m, ws, free, done):
                weighted(m, ws).then_inc(free, 1)
                dve.drain()
                nc.vector.tensor_copy(ws.parts[:, m, 0, :], ws.full)
                dve.drain()
                other_parts(m, ws).then_inc(done, 1)

            def prep_job(name, arg, u, p, jobs, ws, s):
                dve.wait_ge(s.filled, jobs.filled(name, arg))
                if name == "xT":
                    nc.vector.tensor_copy(ws.xT, ws.bank).then_inc(s.free, 1)
                elif name == "qkv":
                    nc.vector.tensor_tensor(ws.qk[:, arg, :], ws.bank[:, 0:2 * D], bqkv_b[:, 0:2 * D], ALU.add)
                    nc.vector.tensor_tensor(v_all[:, bass.ds(u * T + arg, 1), :],
                                            ws.bank[:, 2 * D:3 * D].unsqueeze(1),
                                            bqkv_b[:, 2 * D:3 * D].unsqueeze(1), ALU.add).then_inc(s.free, 1)
                elif name == "kT":
                    need(dve, s.k_stored, (p + s.early) * K_STORED)
                    split(arg, ws, s.free, s.k_split)
                else:
                    need(dve, s.q_stored, (p + s.early) * Q_STORED)
                    split(arg, ws, s.free, s.q_split)

            def ffn_job(name, arg, u, jobs):
                dve.wait_ge(main.filled, jobs.filled(name, arg))
                if name == "gate":
                    nc.vector.tensor_copy(gate[:, arg, :], misc_ap).then_inc(main.free, 1)
                elif name == "up":
                    dve.wait_ge(gate_tanh_done, u + 1)
                    nc.vector.scalar_tensor_tensor(tanh_gate[:, arg, :], tanh_gate[:, arg, :], 1.0, gate[:, arg, :],
                                                   ALU.add, ALU.mult)
                    dve.drain()
                    nc.vector.scalar_tensor_tensor(gate[:, arg, :], tanh_gate[:, arg, :], 0.5, misc_ap,
                                                   ALU.mult, ALU.mult).then_inc(main.free, 1)
                else:
                    nc.vector.tensor_copy(y[:], misc_ap).then_inc(main.free, 1)

            def early_gates(unit):
                dve.wait_ge(gate_tanh_done, unit + 1)
                nc.vector.scalar_tensor_tensor(tanh_gate[:], tanh_gate[:], 1.0, gate_banks, ALU.add, ALU.mult
                                               ).then_inc(ffn_free, 1)
                dve.drain()

            def early_ups(unit):
                dve.wait_ge(ffn_filled, 2 * unit + 2)
                for c in range(HC):
                    last = nc.vector.scalar_tensor_tensor(gate[:, c, :], tanh_gate[:, c, :], 0.5, up_banks[c],
                                                          ALU.mult, ALU.mult)
                last.then_inc(ffn_free, 1)

            def gate_of_y(u):
                dve.wait_ge(y_tanh_done, u + 1)
                tiles = [t[:].rearrange("p (t c) -> p t c", t=T) for t in (tanh_y, y)]
                nc.vector.scalar_tensor_tensor(g2_all[:, bass.ds(u * T, T), :], tiles[0], 1.0, tiles[1],
                                               ALU.add, ALU.mult)
                dve.drain()

            def take_heads(q, i):
                dve.wait_ge(probs_used, i * STEPS + KT * (q + 1))
                nc.vector.transpose(heads_t[:].rearrange("p b m -> p (b m)"), heads_o[:]).then_inc(o_free, 1)
                dve.drain()
                nc.vector.reciprocal(denom_r[:], heads_t[:, :, HD])
                dve.drain()
                nc.vector.tensor_tensor(attn[:, :, q * HD:(q + 1) * HD], heads_t[:, :, 0:HD],
                                        denom_r[:].unsqueeze(2).broadcast_to([P, BLOCKS, HD]), ALU.mult)
                dve.drain()
                if q == QUADS - 1:
                    nc.vector.transpose(attnT, attn.rearrange("p b c -> p (b c)")).then_inc(attn_ready, 1)

            def join(i, jobs):
                dve.wait_ge(main.filled, jobs.filled("proj"))
                tiles = bass.ds((i - 1) * T, T)
                joined_t = joined.rearrange("p (t c) -> p t c", t=T)
                nc.vector.tensor_tensor(joined_t, misc[:].rearrange("p (t c) -> p t c", t=T),
                                        bproj_b[:].unsqueeze(1).broadcast_to([P, T, D]), ALU.add
                                        ).then_inc(main.free, 1)
                dve.drain()
                nc.vector.scalar_tensor_tensor(joined_t, joined_t, 0.5, g2_all[:, tiles, :], ALU.mult, ALU.mult)
                dve.drain()
                dve.wait_ge(out_stored, i * 16)
                nc.vector.tensor_tensor(joined_x[:], joined_t, x_all[:, tiles, :], ALU.add).then_inc(out_ready, 1)

            nc.vector.memset(zeros, 0.0).then_inc(zeros_set, 1)
            dve.wait_ge(norm_loaded, 2 * 16)
            nc.vector.tensor_tensor(bound[0:1, 0:HD], norm_rows[0:1, 0, :], norm_rows[0:1, 1, :], ALU.mult)
            dve.drain()
            nc.vector.tensor_reduce(bound[0:1, HD:HD + 1], bound[0:1, 0:HD], AX_X, ALU.max,
                                    apply_absolute_value=True)
            dve.drain()
            nc.vector.tensor_scalar(bound[0:1, HD + 1:HD + 2], bound[0:1, HD:HD + 1],
                                    -1.0 if force_general else SAFE_BOUND / HD ** 0.5, None, ALU.is_le)
            dve.drain()
            nc.vector.tensor_scalar(unsafe[:], bound[0:1, HD + 1:HD + 2], -1.0, 1.0, ALU.mult, ALU.add
                                    ).then_inc(bound_ready, 1)

            dve.wait_ge(x_first, 2 * 16)
            x_sums(range(2 * T))
            x_rsqrt(range(2 * T))

            def run_general():
                dve.wait_ge(w_loaded, W_DMAS * 16)
                nc.vector.engine_nop().then_inc(general.free, 1)
                nc.vector.engine_nop().then_inc(g_shift, 1)
                dve.wait_ge(x_rest, (UNITS - 2) * 16)
                x_sums(range(2 * T, UNITS * T))
                x_rsqrt(range(2 * T, UNITS * T))
                with dve.Fori(0, UNITS) as u:
                    norm_x(u, first_ws, general)
                    jobs = Jobs(GENERAL_JOBS, u * N_GENERAL)
                    for name, arg in jobs.order:
                        prep_job(name, arg, u, u, jobs, first_ws, general)
                        if (name, arg) == ("qkv", T - 1):
                            for piece in range(5):
                                rms(piece, u, general)
                with dve.Fori(0, UNITS * H) as n:
                    for t in range(T):
                        dve.wait_ge(g_scores, n * T + t + 1)
                        nc.vector.tensor_reduce(row_max[:, t:t + 1], scores[:, t % 2, :, :], AX_XY, ALU.max
                                                ).then_inc(g_max, 1)
                    dve.drain()
                    dve.wait_ge(g_stored, (n + 1) * (PARTS * 16))
                    nc.vector.tensor_scalar(shift_parts[:, 0, :], row_max[:], -1.0, None, ALU.mult)
                    dve.drain()
                    nc.vector.scalar_tensor_tensor(shift_rest[:], row_max[:], -1.0, shift_parts[:, 0, :],
                                                   ALU.mult, ALU.subtract)
                    dve.drain()
                    nc.vector.tensor_copy(shift_parts[:, 1, :], shift_rest[:])
                    dve.drain()
                    nc.vector.tensor_tensor(shift_parts[:, 2, :], shift_rest[:], shift_parts[:, 1, :],
                                            ALU.subtract).then_inc(g_shift, 1)
                dve.drain().then_inc(g_over, 1)

            general_path(dve, run_general)

            def first_job(name, arg):
                prep_job(name, arg, 0, 0, first_jobs, first_ws, main)

            def second_job(name, arg):
                prep_job(name, arg, 1, 0, second_jobs, second_ws, second)

            def early_weighted(name, m, jobs, ws, s):
                dve.wait_ge(s.filled, jobs.filled(name, m))
                weighted(m, ws).then_inc(s.free, 1)
                dve.drain().then_inc(full_ready, 1)

            def early_parts(n, m, ws, done):
                dve.wait_ge(part_ready, n + 1)
                other_parts(m, ws, early_k=m == 1).then_inc(done, 1)
                dve.drain()

            norm_x(0, first_ws, main)
            norm_x(1, second_ws, second)
            dve.wait_ge(w_loaded, W_DMAS * 16)
            first_job("xT", 0)
            second_job("xT", 0)
            for t in range(T):
                first_job("qkv", t)
                second_job("qkv", t)
            sum_squares(0, first_ws, main)
            sum_squares(0, second_ws, second)
            nc.vector.tensor_scalar(rs_x[:], rs_t[:], 1.0 / HD, RMS_EPS, ALU.mult, ALU.add)
            dve.drain()
            rsqrt(rs_x[:], rs_y[:], rs_t[:])
            nc.vector.engine_nop().then_inc(main.rms_ready, 1)
            nc.vector.engine_nop().then_inc(second.rms_ready, 1)
            early_gates(0)
            early_weighted("qT", 0, first_jobs, first_ws, main)
            early_weighted("kT", 1, second_jobs, second_ws, second)
            early_parts(0, 0, first_ws, main.q_split)
            early_weighted("kT", 1, first_jobs, first_ws, main)
            early_ups(0)
            early_parts(2, 1, first_ws, main.k_split)
            early_gates(1)
            dve.wait_ge(second.k_split, 1)
            early_weighted("qT", 0, second_jobs, second_ws, second)
            ffn_job("down", 0, 0, first_jobs)
            early_ups(1)
            gate_of_y(0)
            dve.wait_ge(x_rest, (UNITS - 2) * 16)
            x_sums(range(2 * T, 3 * T))
            x_rsqrt(range(2 * T, 3 * T))
            ffn_job("down", 1, 1, first_jobs)

            def body(i, jobs, post, prep, first):
                for n in range(STEPS):
                    if n == 0 and post:
                        take_heads(QUADS - 1, i - 1)
                    if n == 0 and prep:
                        norm_x(i + 2, first_ws, main)
                        dve.drain()
                    if n and n % KT == 0:
                        if n == KT and first:
                            dve.wait_ge(second.k_stored, K_STORED)
                            dve.wait_ge(second.q_stored, Q_STORED)
                        take_heads(n // KT - 1, i)
                    for name, arg in jobs.at(n):
                        if (n, name, arg) in PREP_JOBS:
                            prep_job(name, arg, i + 2, i + 1, jobs, first_ws, main)
                        elif name == "proj":
                            join(i, jobs)
                        else:
                            ffn_job(name, arg, i + 2, jobs)
                    if prep and n == X_T_STEP:
                        transposed_x()
                    elif prep and n == K_T_STEP:
                        transposed_qk(1, i + 1)
                    elif prep and n == K_SPLIT_STEP:
                        split_transposed(1, main.k_stored, (i + 1) * K_STORED, main.k_split)
                    elif prep and n == Q_T_STEP:
                        transposed_qk(0, i + 1)
                    elif prep and n == Q_SPLIT_STEP:
                        split_transposed(0, main.q_stored, (i + 1) * Q_STORED, main.q_split)
                    if n in RMS_STEPS and prep:
                        for piece in RMS_STEPS[n]:
                            rms(piece, i + 1, main)
                    if first and n == LATE_G2_STEP:
                        gate_of_y(1)
                    if first and n in X_STATS_STEPS:
                        half = (UNITS - 3) * T // 2
                        if n == X_STATS_STEPS[0]:
                            x_sums(range(3 * T, 3 * T + half))
                        elif n == X_STATS_STEPS[1]:
                            x_sums(range(3 * T + half, UNITS * T))
                        else:
                            x_rsqrt(range(3 * T, UNITS * T))
                if prep:
                    gate_of_y(i + 2)

            run_bodies(dve, body)
            take_heads(QUADS - 1, UNITS - 1)
            join(UNITS, LAST_JOBS)


def kernel(**inputs):
    import numpy as np
    import concourse.bacc as bacc
    from concourse.bass_utils import run_bass_kernel_spmd

    w_down = inputs["L0_ffn_w_down"]
    laid_out = {
        "x": inputs["L0_attn_x"],
        "WqkvT": inputs["L0_attn_Wqkv"].T,
        "bqkv": inputs["L0_attn_bqkv"],
        "WprojT": np.asarray(inputs["L0_attn_Wproj"]).T.reshape(QUADS, 4, HD, D).transpose(1, 0, 2, 3).reshape(D, D),
        "bproj": inputs["L0_attn_bproj"],
        "qn_w": np.tile(np.asarray(inputs["L0_attn_qn_w"]), H)[None, :],
        "kn_w": np.tile(np.asarray(inputs["L0_attn_kn_w"]), H)[None, :],
        "w_gateT": inputs["L0_ffn_w_gate"].T,
        "w_upT": inputs["L0_ffn_w_up"].T,
        "w_downT": np.asarray(w_down).reshape(D, HC, P).transpose(2, 1, 0).reshape(P, HC * D),
    }
    nc = bacc.Bacc("TRN2", target_bir_lowering=False, num_devices=1)
    arrays, args = {}, []
    for name, a in laid_out.items():
        a = np.ascontiguousarray(a)
        arrays[f"in_{name}"] = a
        args.append(nc.dram_tensor(f"in_{name}", a.shape, mybir.dt.from_np(a.dtype), kind="ExternalInput").ap())
    out = nc.dram_tensor("out_0", (B, S, D), F32, kind="ExternalOutput").ap()
    attention_ffn(nc, *args, out)
    r = run_bass_kernel_spmd(nc, [arrays], core_ids=[0])
    return r.results[0]["out_0"]
```
